# Optimizing a Trainium2 kernel written in Bass

```python
import numpy as np
import jax
import jax.numpy as jnp

def _softmax(x, axis=-1):
    return jax.nn.softmax(x, axis=axis)

def _gelu(x):
    return jax.nn.gelu(x, approximate=True)

def _silu(x):
    return jax.nn.silu(x)

def _sigmoid(x):
    return jax.nn.sigmoid(x)

def _layernorm(x, axis=-1, eps=1e-05):
    m = jnp.mean(x, axis=axis, keepdims=True)
    v = jnp.var(x, axis=axis, keepdims=True)
    return (x - m) / jnp.sqrt(v + eps)

def _scatter_add(tgt, idx, src, axis=0):
    return tgt.at[idx].add(src)

def _segment_sum(src, seg, n):
    return jax.ops.segment_sum(src, seg, n)
kernel_name = 'mk_adj_preln_d1_adj_r2_b7f4cd'

def setup_inputs(seed: int=0):
    np.random.seed(seed)
    _w = jnp.asarray

    def _rec_inputs():
        import jax
        import jax.numpy as jnp
        _gk = jax.random.key(seed)
        x = -0.0005207 + 1.001 * jax.random.normal(jax.random.fold_in(_gk, 1), (4096, 128), jnp.float32)
        _a = jax.random.bernoulli(jax.random.fold_in(_gk, 2), 0.00195312, (4096, 4096))
        _a = jnp.logical_or(_a, jnp.swapaxes(_a, -1, -2))
        _a = jnp.logical_or(_a, jnp.eye(4096, dtype=bool))
        _af = _a.astype(jnp.float32)
        adj = _af
        return (x, adj)
    x, adj = _rec_inputs()

    def _L0_gnn_setup():
        import jax, jax.numpy as jnp
        import numpy as np
        N = 4096
        EMB = 128
        EDGE_P = 0.004
        LN_EPS = 1e-05

        def _layernorm(h, g, b):
            mu = jnp.mean(h, axis=-1, keepdims=True)
            var = jnp.mean(jnp.square(h - mu), axis=-1, keepdims=True)
            return (h - mu) * jax.lax.rsqrt(var + LN_EPS) * g + b
        key = jax.random.key(seed)
        ks = jax.random.split(key, 10)
        x = jax.random.normal(ks[0], (N, EMB), dtype=jnp.float32)
        adj = (jax.random.uniform(ks[1], (N, N)) < EDGE_P).astype(jnp.float32)
        adj = jnp.fill_diagonal(adj, 1.0, inplace=False)
        s = 1.0 / np.sqrt(EMB)
        W1 = jax.random.normal(ks[2], (EMB, EMB), dtype=jnp.float32) * s
        b1 = jax.random.normal(ks[3], (EMB,), dtype=jnp.float32) * s
        W2 = jax.random.normal(ks[4], (EMB, EMB), dtype=jnp.float32) * s
        b2 = jax.random.normal(ks[5], (EMB,), dtype=jnp.float32) * s
        W3 = jax.random.normal(ks[6], (EMB, EMB), dtype=jnp.float32) * s
        b3 = jax.random.normal(ks[7], (EMB,), dtype=jnp.float32) * s
        ones = jnp.ones((EMB,), jnp.float32)
        zeros = jnp.zeros((EMB,), jnp.float32)
        return {'x': x, 'adj': adj, 'W1': W1, 'b1': b1, 'W2': W2, 'b2': b2, 'W3': W3, 'b3': b3, 'g1': ones, 'be1': zeros, 'g2': ones, 'be2': zeros, 'g3': ones, 'be3': zeros}
    _L0_gnn_all = _L0_gnn_setup()
    _L0_gnn_in = {k: v for k, v in _L0_gnn_all.items() if k in ('W1', 'b1', 'W2', 'b2', 'W3', 'b3', 'g1', 'be1', 'g2', 'be2', 'g3', 'be3')}
    del _L0_gnn_all
    return {'x': x, 'adj': adj, 'L0_gnn_W1': _L0_gnn_in['W1'], 'L0_gnn_b1': _L0_gnn_in['b1'], 'L0_gnn_W2': _L0_gnn_in['W2'], 'L0_gnn_b2': _L0_gnn_in['b2'], 'L0_gnn_W3': _L0_gnn_in['W3'], 'L0_gnn_b3': _L0_gnn_in['b3'], 'L0_gnn_g1': _L0_gnn_in['g1'], 'L0_gnn_be1': _L0_gnn_in['be1'], 'L0_gnn_g2': _L0_gnn_in['g2'], 'L0_gnn_be2': _L0_gnn_in['be2'], 'L0_gnn_g3': _L0_gnn_in['g3'], 'L0_gnn_be3': _L0_gnn_in['be3']}

def reference(x, adj, L0_gnn_W1, L0_gnn_b1, L0_gnn_W2, L0_gnn_b2, L0_gnn_W3, L0_gnn_b3, L0_gnn_g1, L0_gnn_be1, L0_gnn_g2, L0_gnn_be2, L0_gnn_g3, L0_gnn_be3):
    import jax
    import jax.numpy as jnp

    def _L0_gnn_ref(x, adj, W1, b1, W2, b2, W3, b3, g1, be1, g2, be2, g3, be3):
        import jax, jax.numpy as jnp
        import numpy as np
        N = 4096
        EMB = 128
        EDGE_P = 0.004
        LN_EPS = 1e-05

        def _layernorm(h, g, b):
            mu = jnp.mean(h, axis=-1, keepdims=True)
            var = jnp.mean(jnp.square(h - mu), axis=-1, keepdims=True)
            return (h - mu) * jax.lax.rsqrt(var + LN_EPS) * g + b
        dinv = jnp.sum(adj, axis=-1) ** (-0.5)
        A = adj * dinv[:, None] * dinv[None, :]
        h1 = x @ W1 + b1
        n1 = _layernorm(jax.nn.relu(A @ h1) + h1, g1, be1)
        h2 = n1 @ W2 + b2
        n2 = _layernorm(jax.nn.relu(A @ h2) + n1, g2, be2)
        h3 = n2 @ W3 + b3
        n3 = _layernorm(jax.nn.relu(A @ h3) + n2, g3, be3)
        return n3
    h = jnp.maximum(_layernorm(x, axis=-1), 0.0)
    x = x + _L0_gnn_ref(h, adj, L0_gnn_W1, L0_gnn_b1, L0_gnn_W2, L0_gnn_b2, L0_gnn_W3, L0_gnn_b3, L0_gnn_g1, L0_gnn_be1, L0_gnn_g2, L0_gnn_be2, L0_gnn_g3, L0_gnn_be3)
    return x

_drawn_inputs = setup_inputs


def setup_inputs(seed=0):
    import zlib

    import numpy as np

    out = dict(_drawn_inputs(seed))
    spreads = {'L0_gnn_g1': (1.0, 0.2),
     'L0_gnn_be1': (0.0, 0.1),
     'L0_gnn_g2': (1.0, 0.2),
     'L0_gnn_be2': (0.0, 0.1),
     'L0_gnn_g3': (1.0, 0.2),
     'L0_gnn_be3': (0.0, 0.1)}
    factors = {}
    for name, (base, spread) in spreads.items():
        noise = np.random.default_rng([zlib.crc32(name.encode()), seed]).standard_normal(out[name].shape)
        drawn = base * np.exp(spread * noise) if base else spread * noise
        out[name] = jnp.asarray(drawn.astype(out[name].dtype))
    for name, factor in factors.items():
        out[name] = (out[name] * factor).astype(out[name].dtype)
    return out
```

```python
from contextlib import ExitStack

import concourse.bass as bass
from concourse import mybir

FP32 = mybir.dt.float32
FP16 = mybir.dt.float16
FP8 = mybir.dt.float8e4
FP8W = mybir.dt.float8e5
I32 = mybir.dt.int32
ALU = mybir.AluOpType
ACT = mybir.ActivationFunctionType
AX = mybir.AxisListType

P = 128
N = 4096
E = 128
T = N // P
CW = 512
NC = N // CW
TC = CW // P
LAYERS = 3
EPS = 1e-5
HS_SCALE = 4096.0

UNIT = 2048
UPB = N // UNIT
UNITS = T * UPB
SLOTS = 4
NA = 6
PRO_BANK, SYM_BANK = 6, 7
XPARTS = 4

DIGITS = 8
GROUPS = []
_used = DIGITS + 1
for _k in range(T):
    _need = _k // TC + 1
    if _used + _need > DIGITS:
        GROUPS.append([])
        _used = 0
    GROUPS[-1].append((_k, _used))
    _used += _need
GROUP_ENDS = {g[-1][0]: n for n, g in enumerate(GROUPS)}
GROUP_STARTS = {g[0][0]: n for n, g in enumerate(GROUPS)}
FIRST_DIGIT = {k: d for g in GROUPS for k, d in g}

EV_EXACT = 0
EV_SYM = EV_EXACT + UNITS
EV_LO = EV_SYM + len(GROUPS)
EV_END = EV_LO + LAYERS * T

_NORM = ["y", "stats", "moments", "variance", "rstd", "centred"]
_NEXT = ["n_transposed", "nT_copied", "projected", "h", "h_kept", "h_scaled", "hs_stored"]
_LAYER = ["row_transposed", "rowT_copied", "summed", "dinv_fetched", "residual_fetched", "scaled"]
STEPS = ([["dinv_fetched"] + _NORM + ["n"] + _NEXT]
         + [_LAYER + _NORM + ["gained", "n"] + _NEXT] * (LAYERS - 1)
         + [_LAYER + _NORM + ["gained", "n", "result"]])


def tile_begins(stage, i):
    return i * len(STEPS[stage]) + (1 + T * sum(len(STEPS[s]) for s in range(stage)))


def after(stage, i, step):
    return tile_begins(stage, i) + (STEPS[stage].index(step) + 1)


def general_sync(nc, sp, m):
    for stage in range(LAYERS + 1):
        with sp.Fori(0, T) as i:
            sp.wait_ge(m.step, tile_begins(stage, i))
            if stage:
                sp.dma_start(m.row[:, :], m.adj[bass.ts(i, P), :]).then_inc(m.row_in, 16)
            if stage in (0, LAYERS):
                sp.dma_start(m.xt[:, :], m.x[bass.ts(i, P), :]).then_inc(m.x_in, 16)
            if stage == LAYERS:
                sp.wait_ge(m.step, after(stage, i, "result"))
                sp.dma_start(m.out[bass.ts(i, P), :], m.result[:, :]).then_inc(m.stored, 16)
    sp.wait_ge(m.stored, 16 * T)


def general_tensor(nc, pe, m):
    for stage in range(LAYERS + 1):
        with pe.Fori(0, T) as i:
            if stage:
                pe.wait_ge(m.row_in, (i + (stage - 1) * T + 1) * 16)
                for k in range(T):
                    last = nc.tensor.transpose(m.bank[k // TC][:, (k % TC) * P:(k % TC + 1) * P],
                                               m.row[:, k * P:(k + 1) * P], m.ident[:, :])
                last.then_inc(m.step, 1)
                pe.wait_ge(m.step, after(stage, i, "rowT_copied"))
                for k in range(T):
                    last = nc.tensor.matmul(m.bank[0][:, 0:E], m.rowT[:, k, :], m.hs[(stage - 1) % 2][:, k, :],
                                            start=(k == 0), stop=(k == T - 1))
                last.then_inc(m.step, 1)
            if stage < LAYERS:
                pe.wait_ge(m.step, after(stage, i, "n"))
                nc.tensor.transpose(m.bank[1][:, 0:P], m.n[:, :], m.ident[:, :]).then_inc(m.step, 1)
                pe.wait_ge(m.step, after(stage, i, "nT_copied"))
                nc.tensor.matmul(m.bank[2][:, 0:E], m.nT[:, :], m.w[:, stage, :], start=True,
                                 stop=True).then_inc(m.step, 1)


def general_scalar(nc, act, m):
    for stage in range(LAYERS + 1):
        with act.Fori(0, T) as i:
            if stage:
                act.wait_ge(m.step, after(stage, i, "row_transposed"))
                for c in range(NC):
                    last = nc.scalar.activation(m.rowT[:, c * TC:(c + 1) * TC, :], m.tiles(m.bank[c][:, :]), ACT.Copy)
                last.then_inc(m.step, 1)
            if stage < LAYERS:
                act.wait_ge(m.step, after(stage, i, "n_transposed"))
                nc.scalar.activation(m.nT[:, :], m.bank[1][:, 0:P], ACT.Copy).then_inc(m.step, 1)


def general_pool(nc, pool, m):
    for stage in range(LAYERS + 1):
        with pool.Fori(0, T) as i:
            pool.wait_ge(m.step, after(stage, i, "moments"))
            nc.gpsimd.tensor_tensor(m.var[:, :], m.mv[:, 1:2], m.eps[:, :], ALU.add).then_inc(m.step, 1)
            pool.wait_ge(m.step, after(stage, i, "variance"))
            nc.gpsimd.tensor_tensor(m.rstd[:, :], m.var[:, :], m.mhalf[:, 0:1], ALU.pow).then_inc(m.step, 1)


def general_vector(nc, dve, m):
    def carry():
        nc.vector.memset(m.carrier[:, :], 0.0)

    nc.vector.memset(m.eps[:, :], EPS).then_inc(m.step, 1)
    for stage in range(LAYERS + 1):
        with dve.Fori(0, T) as i:
            def then(ins, step):
                ins.then_inc(m.step, 1)
                dve.wait_ge(m.step, after(stage, i, step))

            if stage:
                dve.wait_ge(m.step, after(stage, i, "summed"))
                carry()
                then(nc.vector.tensor_copy(m.dinv_i[:, :], m.dinv[:, bass.ds(i, 1)]), "dinv_fetched")
                carry()
                then(nc.vector.tensor_copy(m.res_i[:, :], m.res[:, bass.ds(i, 1), :]), "residual_fetched")
                then(nc.vector.tensor_scalar(m.y[:, :], m.bank[0][:, 0:E], m.dinv_i[:, :], 0.0, ALU.mult, ALU.max),
                     "scaled")
                then(nc.vector.tensor_tensor(m.y[:, :], m.y[:, :], m.res_i[:, :], ALU.add), "y")
            else:
                dve.wait_ge(m.x_in, (i + 1) * 16)
                dve.wait_ge(m.step, tile_begins(stage, i))
                carry()
                then(nc.vector.tensor_copy(m.dinv_i[:, :], m.dinv[:, bass.ds(i, 1)]), "dinv_fetched")
                then(nc.vector.tensor_copy(m.y[:, :], m.xt[:, :]), "y")
            then(nc.vector.bn_stats(m.st[:, :], m.y[:, :]), "stats")
            carry()
            then(nc.vector.bn_aggr(m.mv[:, :], m.st[:, :]), "moments")
            dve.wait_ge(m.step, after(stage, i, "rstd"))
            then(nc.vector.tensor_scalar(m.y[:, :], m.y[:, :], m.mv[:, 0:1], m.rstd[:, :], ALU.subtract, ALU.mult),
                 "centred")
            if stage:
                then(nc.vector.tensor_tensor(m.y[:, :], m.y[:, :], m.g[:, stage - 1, :], ALU.mult), "gained")
                then(nc.vector.tensor_tensor(m.n[:, :], m.y[:, :], m.be[:, stage - 1, :], ALU.add), "n")
            else:
                then(nc.vector.tensor_scalar(m.n[:, :], m.y[:, :], 0.0, None, ALU.max), "n")
            if stage < LAYERS:
                dve.wait_ge(m.step, after(stage, i, "projected"))
                then(nc.vector.tensor_tensor(m.h[:, :], m.bank[2][:, 0:E], m.b[:, stage, :], ALU.add), "h")
                kept = m.n if stage else m.h
                carry()
                then(nc.vector.tensor_copy(m.res[:, bass.ds(i, 1), :], kept[:, :]), "h_kept")
                then(nc.vector.tensor_scalar(m.h[:, :], m.h[:, :], m.dinv_i[:, :], None, ALU.mult), "h_scaled")
                carry()
                then(nc.vector.tensor_copy(m.hs[stage % 2][:, bass.ds(i, 1), :], m.h[:, :]), "hs_stored")
            else:
                dve.wait_ge(m.x_in, (i + T + 1) * 16)
                then(nc.vector.tensor_tensor(m.result[:, :], m.n[:, :], m.xt[:, :], ALU.add), "result")


def build(nc, x, adj, w, b, g, be, out):
    x_v = x.rearrange("(t p) e -> p t e", p=P)
    out_v = out.rearrange("(t p) e -> p t e", p=P)
    adj_v = adj.rearrange("(t p) n -> t p n", p=P)

    ctx = ExitStack()
    with ctx:
        def sb(name, shape, dt):
            return ctx.enter_context(nc.sbuf_tensor(name, shape, dt))

        def sem(name):
            return ctx.enter_context(nc.semaphore(name))

        adj8 = sb("adj8", [P, T, N], FP8)
        stage = sb("stage", [P, SLOTS * UNIT], FP32)
        nres = sb("nres", [P, T, E], FP32)
        hs_a = sb("hs_a", [P, T, 2, E], FP16)
        ident = sb("ident", [P, P], FP32)
        wplus = sb("wplus", [P, DIGITS, P], FP8W)
        wminus = sb("wminus", [P, DIGITS, P], FP8W)
        zeros = sb("zeros", [P, P], FP8W)
        w_sb = sb("w_sb", [P, LAYERS, E], FP32)
        b_bc = sb("b_bc", [P, LAYERS, E], FP32)
        g_bc = sb("g_bc", [P, LAYERS, E], FP32)
        be_bc = sb("be_bc", [P, LAYERS, E], FP32)
        junk = sb("junk", [P, 2, UNIT], FP8)
        evidence = sb("evidence", [P, EV_END], FP32)
        rs_part = sb("rs_part", [P, T, UPB], FP32)
        rowsum = sb("rowsum", [P, T], FP32)
        dinv = sb("dinv", [P, T], FP32)
        dinv_in = sb("dinv_in", [P, T], FP32)
        dinv_out = sb("dinv_out", [P, T], FP32)
        mhalf = sb("mhalf", [P, TC], FP32)
        ones = sb("ones", [P, 1], FP32)
        st0 = sb("st0", [P, TC, 6], FP32)
        mv0 = sb("mv0", [P, TC, 2], FP32)
        var0 = sb("var0", [P, TC], FP32)
        rstd0 = sb("rstd0", [P, T], FP32)
        st = sb("st", [P, TC, 6], FP32)
        mv = sb("mv", [P, 2, TC, 2], FP32)
        vare = sb("vare", [P, 2, TC], FP32)
        rstd = sb("rstd", [P, 2, TC], FP32)
        ev_sum = sb("ev_sum", [P, 1], FP32)
        clean = sb("clean", [1, 1], I32)

        x_sb = adj8[:, T - 4:T, :].rearrange("p a n -> p (a n)").bitcast(FP32).rearrange("p (t e) -> p t e", e=E)
        xT = adj8[:, T - 5:T - 4, :].rearrange("p a n -> p (a n)").bitcast(FP32).rearrange("p (s n) -> p s n", n=CW)
        hs_b = stage[:, 0:N].bitcast(FP16).rearrange("p (t h e) -> p t h e", h=2, e=E)
        xb = stage[:, 0:N].rearrange("p (t e) -> p t e", e=E)

        def epi(n):
            return stage[:, N + 2 * n * CW:N + 2 * (n + 1) * CW].rearrange("p (s n) -> p s n", n=CW)

        reluT, nT, yb, hb = epi(0), epi(1), epi(2), epi(3)
        hs_of = [hs_a, hs_b, hs_a]

        bank = [ctx.enter_context(nc.psum_tensor(f"bank{i}", [P, CW], FP32)) for i in range(NC)]

        def tiles(ap):
            return ap.rearrange("p (t e) -> p t e", e=E)

        x_in = [sem(f"x_in{i}") for i in range(XPARTS)]
        params_in = sem("params_in")
        x_again = sem("x_again")
        slot_in = [sem(f"slot_in{i}") for i in range(SLOTS)]
        ident_0 = sem("ident_0")
        ident_ok = sem("ident_ok")
        const_ok = sem("const_ok")
        converted = sem("converted")
        checked = sem("checked")
        pool_step = sem("pool_step")
        dinv_ok = sem("dinv_ok")
        dout_ok = sem("dout_ok")
        stat0 = sem("stat0")
        mv0_ok = sem("mv0_ok")
        rstd0_ok = sem("rstd0_ok")
        relu0_ok = sem("relu0_ok")
        xT_ps = sem("xT_ps")
        xT_ok = sem("xT_ok")
        h1_ps = sem("h1_ps")
        h1_ok = sem("h1_ok")
        hi1_ok = sem("hi1_ok")
        lo1_ok = sem("lo1_ok")
        sym_ps = sem("sym_ps")
        sym_read = sem("sym_read")
        acc_done = sem("acc_done")
        relu_ok = sem("relu_ok")
        back_ps = sem("back_ps")
        y_ok = sem("y_ok")
        stat_ok = sem("stat_ok")
        mv_ok = sem("mv_ok")
        rstd_ok = sem("rstd_ok")
        z_ok = sem("z_ok")
        zg_ok = sem("zg_ok")
        n_ok = sem("n_ok")
        nT_ps = sem("nT_ps")
        nT_ok = sem("nT_ok")
        h_ps = sem("h_ps")
        h_ok = sem("h_ok")
        hi_ok = sem("hi_ok")
        lo_ok = sem("lo_ok")
        xb_ok = sem("xb_ok")
        ev_step = sem("ev_step")
        ev_ps = sem("ev_ps")
        clean_ok = sem("clean_ok")
        out_done = sem("out_done")

        class General:
            pass

        m = General()
        taken = [0]

        def room(cols):
            first = taken[0]
            taken[0] += cols
            return adj8[:, :, :].rearrange("p t n -> p (t n)").bitcast(FP32)[:, first:taken[0]]

        m.x, m.adj, m.out = x, adj, out
        m.row = room(N)
        m.rowT = room(N).rearrange("p (t n) -> p t n", n=P)
        m.hs = [room(N).rearrange("p (t n) -> p t n", n=E) for _ in range(2)]
        m.xt, m.y, m.res_i, m.n, m.nT, m.h, m.result = (room(E) for _ in range(7))
        m.dinv_i, m.var, m.rstd, m.eps, m.carrier = (room(1) for _ in range(5))
        m.st, m.mv = room(6), room(2)
        m.res, m.dinv, m.ident, m.mhalf = nres, dinv, ident, mhalf
        m.w, m.b, m.g, m.be, m.bank, m.tiles = w_sb, b_bc, g_bc, be_bc, bank, tiles
        m.step = sem("general_step")
        m.row_in = sem("general_row_in")
        m.x_in = sem("general_x_in")
        m.stored = sem("general_stored")

        def unless_clean(eng):
            eng.wait_ge(clean_ok, 1)
            verdict = eng.alloc_register()
            eng.reg_load(verdict, clean[0:1, 0:1])
            return eng.If_eq(verdict, 0)

        block = ctx.enter_context(nc.Block())

        @block.sync
        def _(sp):
            for u in range(UNITS):
                s = u % SLOTS
                if u >= SLOTS:
                    sp.wait_ge(converted, u - SLOTS + 1)
                    sp.wait_ge(checked, u - SLOTS + 1)
                c0 = (u % UPB) * UNIT
                sp.dma_start(stage[:, s * UNIT:(s + 1) * UNIT],
                             adj_v[u // UPB, :, c0:c0 + UNIT]).then_inc(slot_in[s], 16)
            sp.wait_ge(acc_done, 2 * NC)
            sp.dma_start(xb, x_v).then_inc(x_again, 16)
            for c in range(NC):
                sp.wait_ge(n_ok, 2 * NC + c + 1)
                sp.dma_start(out_v[:, c * TC:(c + 1) * TC, :],
                             nres[:, c * TC:(c + 1) * TC, :]).then_inc(out_done, 16)
            sp.wait_ge(out_done, 16 * NC)
            with unless_clean(sp):
                general_sync(nc, sp, m)

        @block.gpsimd
        def _(pool):
            steps = [0]

            def chain(ins):
                steps[0] += 1
                ins.then_inc(pool_step, 1)
                pool.wait_ge(pool_step, steps[0])

            nc.gpsimd.memset(ident[:, :], 0.0).then_inc(ident_0, 1)
            nc.gpsimd.memset(mhalf[:, :], -0.5)
            nc.gpsimd.memset(ones[:, :], 1.0)
            pool.wait_ge(ident_0, 1)
            nc.gpsimd.affine_select(out=ident[:, :], in_=ident[:, :], compare_op=ALU.not_equal, fill=1.0,
                                    base=0, pattern=[[-1, P]], channel_multiplier=1).then_inc(ident_ok, 1)
            pool.wait_ge(ident_ok, 1)

            def rstd_of_x(i):
                pool.wait_ge(mv0_ok, i + 1)
                chain(nc.gpsimd.tensor_scalar(var0[:, :], mv0[:, :, 1], EPS, None, ALU.add))
                nc.gpsimd.tensor_tensor(rstd0[:, i * TC:(i + 1) * TC], var0[:, :], mhalf[:, :],
                                        ALU.pow).then_inc(rstd0_ok, 1)

            rstd_of_x(0)
            for k in range(T):
                if k % TC == 0 and k // TC + 1 < NC:
                    rstd_of_x(k // TC + 1)
                pool.wait_ge(converted, UPB * (k + 1))
                chain(nc.gpsimd.tensor_tensor(rowsum[:, k:k + 1], rs_part[:, k, 0:1], rs_part[:, k, 1:2], ALU.add))
                chain(nc.gpsimd.tensor_tensor(dinv[:, k:k + 1], rowsum[:, k:k + 1], mhalf[:, 0:1], ALU.pow))
                nc.gpsimd.tensor_scalar(dinv_in[:, k:k + 1], dinv[:, k:k + 1], HS_SCALE, None,
                                        ALU.mult).then_inc(dinv_ok, 1)
            nc.gpsimd.tensor_scalar(dinv_out[:, :], dinv[:, :], 1.0 / HS_SCALE, None, ALU.mult).then_inc(dout_ok, 1)

            for q in range(LAYERS * NC):
                pool.wait_ge(mv_ok, q + 1)
                if q >= 2:
                    pool.wait_ge(z_ok, q - 1)
                chain(nc.gpsimd.tensor_scalar(vare[:, q % 2, :], mv[:, q % 2, :, 1], EPS, None, ALU.add))
                nc.gpsimd.tensor_tensor(rstd[:, q % 2, :], vare[:, q % 2, :], mhalf[:, :],
                                        ALU.pow).then_inc(rstd_ok, 1)
                if q == 2 * NC:
                    pool.wait_ge(x_again, 16)
                    nc.gpsimd.tensor_tensor(xb, xb, be_bc[:, LAYERS - 1:LAYERS, :].to_broadcast([P, T, E]),
                                            ALU.add).then_inc(xb_ok, 1)
            with unless_clean(pool):
                general_pool(nc, pool, m)

        @block.scalar
        def _(act):
            tx = T // XPARTS
            for i in range(XPARTS):
                act.dma_start(x_sb[:, i * tx:(i + 1) * tx, :], x_v[:, i * tx:(i + 1) * tx, :]).then_inc(x_in[i], 16)
                if i == 0:
                    for l in range(LAYERS):
                        act.dma_start(w_sb[:, l, :], w[l]).then_inc(params_in, 16)
                        act.dma_start(b_bc[:, l, :], b[l].partition_broadcast(P)).then_inc(params_in, 16)
                        act.dma_start(g_bc[:, l, :], g[l].partition_broadcast(P)).then_inc(params_in, 16)
                        act.dma_start(be_bc[:, l, :], be[l].partition_broadcast(P)).then_inc(params_in, 16)

            def convert(u):
                s, k, c0 = u % SLOTS, u // UPB, (u % UPB) * UNIT
                act.wait_ge(slot_in[s], 16 * (u // SLOTS + 1))
                if k == T - 5:
                    act.wait_ge(h1_ps, NC)
                if k == T - 4:
                    act.wait_ge(xT_ps, NC)
                nc.scalar.activation(adj8[:, k, c0:c0 + UNIT], stage[:, s * UNIT:(s + 1) * UNIT], ACT.Copy,
                                     accum_out=rs_part[:, k, u % UPB:u % UPB + 1],
                                     saturate=False).then_inc(converted, 1)

            def copy_xT(i):
                act.wait_ge(xT_ps, i + 1)
                if i >= 2:
                    act.wait_ge(h1_ps, i - 1)
                nc.scalar.activation(xT[:, i % 2, :], bank[PRO_BANK][:, :], ACT.Copy).then_inc(xT_ok, 1)

            def high_1(k):
                act.wait_ge(dinv_ok, k + 1)
                act.wait_ge(h1_ok, k // TC + 1)
                nc.scalar.activation(hs_a[:, k, 0, :], nres[:, k, :], ACT.Copy,
                                     scale=dinv_in[:, k:k + 1]).then_inc(hi1_ok, 1)

            def read_sym(n):
                act.wait_ge(sym_ps, n + 1)
                nc.scalar.activation(bank[SYM_BANK][:, :], bank[SYM_BANK][:, :], ACT.Abs,
                                     accum_out=evidence[:, EV_SYM + n:EV_SYM + n + 1]).then_inc(sym_read, 1)

            copy_xT(0)
            for k in range(T):
                convert(UPB * k)
                if k:
                    high_1(k - 1)
                convert(UPB * k + 1)
                if k % TC == 1 and k // TC + 1 < NC:
                    copy_xT(k // TC + 1)
                if k and k - 1 in GROUP_ENDS:
                    read_sym(GROUP_ENDS[k - 1])
            high_1(T - 1)
            read_sym(len(GROUPS) - 1)

            def relu_out(q):
                act.wait_ge(acc_done, q + 1)
                if q == 0:
                    act.wait_ge(checked, UNITS)
                if q >= 2:
                    act.wait_ge(back_ps, q - 1)
                nc.scalar.activation(reluT[:, q % 2, :], bank[q % NC][:, :], ACT.Relu).then_inc(relu_ok, 1)

            def copy_nT(q):
                act.wait_ge(nT_ps, q + 1)
                if q >= 2:
                    act.wait_ge(h_ps, q - 1)
                nc.scalar.activation(nT[:, q % 2, :], bank[q % NC][:, :], ACT.Copy).then_inc(nT_ok, 1)

            def high(q):
                act.wait_ge(h_ok, q + 1)
                hs, c = hs_of[q // NC + 1], q % NC
                for t in range(TC):
                    k = c * TC + t
                    last = nc.scalar.activation(hs[:, k, 0, :], tiles(hb[:, q % 2, :])[:, t, :], ACT.Copy,
                                                scale=dinv_in[:, k:k + 1])
                last.then_inc(hi_ok, 1)

            relu_out(0)
            relu_out(1)
            for q in range(NC):
                copy_nT(q)
                if q + 2 < NC:
                    relu_out(q + 2)
                high(q)
            relu_out(NC)
            relu_out(NC + 1)
            for q in (NC, NC + 1):
                copy_nT(q)
                high(q)
            for q in range(NC + 2, 2 * NC):
                relu_out(q)
                copy_nT(q)
                high(q)
            for q in range(2 * NC, 3 * NC):
                relu_out(q)
            with unless_clean(act):
                general_scalar(nc, act, m)

        @block.vector
        def _(dve):
            def check(u):
                s = u % SLOTS
                dve.wait_ge(slot_in[s], 16 * (u // SLOTS + 1))
                if u >= 2:
                    dve.wait_ge(checked, u - 1)
                src = stage[:, s * UNIT:(s + 1) * UNIT]
                nc.vector.scalar_tensor_tensor(out=junk[:, u % 2, :], in0=src, scalar=1.0, in1=src,
                                               op0=ALU.is_equal, op1=ALU.not_equal,
                                               accum_out=evidence[:, EV_EXACT + u:EV_EXACT + u + 1],
                                               saturate=False).then_inc(checked, 1)

            def norm_x(i):
                if i % (NC // XPARTS) == 0:
                    dve.wait_ge(x_in[i // (NC // XPARTS)], 16)
                for t in range(TC):
                    last = nc.vector.bn_stats(st0[:, t, :], x_sb[:, i * TC + t, :])
                last.then_inc(stat0, 1)
                dve.wait_ge(stat0, i + 1)
                if i:
                    dve.wait_ge(rstd0_ok, i)
                for t in range(TC):
                    last = nc.vector.bn_aggr(mv0[:, t, :], st0[:, t, :])
                last.then_inc(mv0_ok, 1)
                dve.wait_ge(mv0_ok, i + 1)
                for t in range(TC):
                    xt = x_sb[:, i * TC + t, :]
                    last = nc.vector.tensor_scalar(xt, xt, mv0[:, t, 0:1], 0.0, ALU.subtract, ALU.max)
                last.then_inc(relu0_ok, 1)

            def h_1(i):
                dve.wait_ge(h1_ps, i + 1)
                dve.wait_ge(rstd0_ok, i + 1)
                for t in range(TC):
                    k = i * TC + t
                    last = nc.vector.scalar_tensor_tensor(out=nres[:, k, :], in0=tiles(bank[PRO_BANK][:, :])[:, t, :],
                                                          scalar=rstd0[:, k:k + 1], in1=b_bc[:, 0, :],
                                                          op0=ALU.mult, op1=ALU.add)
                last.then_inc(h1_ok, 1)

            def low_1(k):
                dve.wait_ge(hi1_ok, k + 1)
                nc.vector.scalar_tensor_tensor(out=hs_a[:, k, 1, :], in0=nres[:, k, :], scalar=dinv_in[:, k:k + 1],
                                               in1=hs_a[:, k, 0, :], op0=ALU.mult, op1=ALU.subtract,
                                               accum_out=evidence[:, EV_LO + k:EV_LO + k + 1]).then_inc(lo1_ok, 1)

            dve.wait_ge(ident_ok, 1)
            nc.vector.memset(zeros[:, :], 0.0)
            for d in range(DIGITS):
                nc.vector.tensor_scalar(wplus[:, d, :], ident[:, :], float(4 ** d), None, ALU.mult, saturate=False)
                last = nc.vector.tensor_scalar(wminus[:, d, :], ident[:, :], -float(4 ** d), None, ALU.mult,
                                               saturate=False)
            last.then_inc(const_ok, 1)
            check(0)
            check(1)
            norm_x(0)
            for k in range(T):
                if k:
                    check(UPB * k)
                    low_1(k - 1)
                    check(UPB * k + 1)
                else:
                    dve.wait_ge(params_in, 16 * 4 * LAYERS)
                    h_1(0)
                if k % TC == 0 and k // TC + 1 < NC:
                    norm_x(k // TC + 1)
                if k % TC == 2 and k // TC + 1 < NC:
                    h_1(k // TC + 1)
            low_1(T - 1)
            dve.wait_ge(dout_ok, 1)

            def residual(q):
                l, c = divmod(q, NC)
                dve.wait_ge(back_ps, q + 1)
                y = tiles(yb[:, q % 2, :])
                for t in range(TC):
                    k = c * TC + t
                    last = nc.vector.scalar_tensor_tensor(out=y[:, t, :], in0=tiles(bank[c][:, :])[:, t, :],
                                                          scalar=dinv_out[:, k:k + 1], in1=nres[:, k, :],
                                                          op0=ALU.mult, op1=ALU.add)
                last.then_inc(y_ok, 1)
                dve.wait_ge(y_ok, q + 1)
                for t in range(TC):
                    last = nc.vector.bn_stats(st[:, t, :], y[:, t, :])
                last.then_inc(stat_ok, 1)
                dve.wait_ge(stat_ok, q + 1)
                if q >= 2:
                    dve.wait_ge(rstd_ok, q - 1)
                for t in range(TC):
                    last = nc.vector.bn_aggr(mv[:, q % 2, t, :], st[:, t, :])
                last.then_inc(mv_ok, 1)

            def normalise(q):
                l, c = divmod(q, NC)
                y = tiles(yb[:, q % 2, :])
                dve.wait_ge(mv_ok, q + 1)
                dve.wait_ge(rstd_ok, q + 1)
                for t in range(TC):
                    last = nc.vector.tensor_scalar(y[:, t, :], y[:, t, :], mv[:, q % 2, t, 0:1],
                                                   rstd[:, q % 2, t:t + 1], ALU.subtract, ALU.mult)
                last.then_inc(z_ok, 1)
                dve.wait_ge(z_ok, q + 1)
                nc.vector.tensor_tensor(y, y, g_bc[:, l:l + 1, :].to_broadcast([P, TC, E]), ALU.mult).then_inc(zg_ok, 1)
                dve.wait_ge(zg_ok, q + 1)
                if l < LAYERS - 1:
                    shift = be_bc[:, l:l + 1, :].to_broadcast([P, TC, E])
                else:
                    dve.wait_ge(xb_ok, 1)
                    shift = xb[:, c * TC:(c + 1) * TC, :]
                nc.vector.tensor_tensor(nres[:, c * TC:(c + 1) * TC, :], y, shift, ALU.add).then_inc(n_ok, 1)

            def bias(q):
                l, c = divmod(q, NC)
                dve.wait_ge(h_ps, q + 1)
                nc.vector.tensor_tensor(tiles(hb[:, q % 2, :]), tiles(bank[c][:, :]),
                                        b_bc[:, l + 1:l + 2, :].to_broadcast([P, TC, E]), ALU.add).then_inc(h_ok, 1)

            def low(q):
                l, c = divmod(q, NC)
                hs = hs_of[l + 1]
                dve.wait_ge(h_ok, q + 1)
                dve.wait_ge(hi_ok, q + 1)
                for t in range(TC):
                    k = c * TC + t
                    ev = EV_LO + (l + 1) * T + k
                    last = nc.vector.scalar_tensor_tensor(out=hs[:, k, 1, :], in0=tiles(hb[:, q % 2, :])[:, t, :],
                                                          scalar=dinv_in[:, k:k + 1], in1=hs[:, k, 0, :],
                                                          op0=ALU.mult, op1=ALU.subtract,
                                                          accum_out=evidence[:, ev:ev + 1])
                last.then_inc(lo_ok, 1)

            for q in range(NC):
                residual(q)
                if q:
                    bias(q - 1)
                normalise(q)
                if q:
                    low(q - 1)
            bias(NC - 1)
            low(NC - 1)
            residual(NC)
            residual(NC + 1)
            normalise(NC)
            normalise(NC + 1)
            for q in (NC, NC + 1):
                bias(q)
                low(q)
            for q in range(NC + 2, 2 * NC):
                residual(q)
                normalise(q)
                bias(q)
                low(q)

            dve.wait_ge(lo_ok, 2 * NC)
            dve.wait_ge(sym_read, len(GROUPS))
            nc.vector.tensor_scalar(evidence[:, EV_LO:EV_END], evidence[:, EV_LO:EV_END], 0.0, None,
                                    ALU.mult).then_inc(ev_step, 1)
            dve.wait_ge(ev_step, 1)
            nc.vector.tensor_reduce(ev_sum[:, :], evidence[:, :], AX.X, ALU.add).then_inc(ev_step, 1)

            for q in range(2 * NC, 3 * NC):
                residual(q)
                normalise(q)
                if q == 2 * NC + 1:
                    dve.wait_ge(ev_ps, 1)
                    nc.vector.tensor_scalar(clean[:, :], bank[NC - 1][0:1, 0:1], 0.0, None,
                                            ALU.is_equal).then_inc(clean_ok, 1)
            with unless_clean(dve):
                dve.wait_ge(out_done, 16 * NC)
                general_vector(nc, dve, m)

        @block.tensor
        def _(pe):
            def transpose_x(i):
                pe.wait_ge(relu0_ok, i + 1)
                if i:
                    pe.wait_ge(h1_ok, i)
                for t in range(TC):
                    last = nc.tensor.transpose(bank[PRO_BANK][:, t * P:(t + 1) * P], x_sb[:, i * TC + t, :], ident[:, :])
                last.then_inc(xT_ps, 1)

            def project_x(i):
                pe.wait_ge(xT_ok, i + 1)
                for t in range(TC):
                    last = nc.tensor.matmul(bank[PRO_BANK][:, t * E:(t + 1) * E], xT[:, i % 2, t * P:(t + 1) * P],
                                            w_sb[:, 0, :], start=True, stop=True)
                last.then_inc(h1_ps, 1)

            def symmetry(k):
                pe.wait_ge(converted, UPB * (k + 1))
                if k in GROUP_STARTS:
                    if GROUP_STARTS[k]:
                        pe.wait_ge(sym_read, GROUP_STARTS[k])
                    nc.tensor.matmul(bank[SYM_BANK][:, :], zeros[:, :], adj8[:, 0, 0:CW],
                                     start=True, stop=False)
                for j0 in range(0, k + 1, TC):
                    d = FIRST_DIGIT[k] + j0 // TC
                    j1 = min(j0 + TC, k + 1)
                    for j in range(j0, j1):
                        nc.tensor.matmul(bank[SYM_BANK][:, (j - j0) * P:(j - j0 + 1) * P],
                                         adj8[:, j, k * P:(k + 1) * P], wplus[:, d, :], start=False, stop=False)
                    last = nc.tensor.matmul(bank[SYM_BANK][:, 0:(j1 - j0) * P], wminus[:, d, :],
                                            adj8[:, k, j0 * P:j1 * P], start=False,
                                            stop=(k in GROUP_ENDS and j1 == k + 1))
                if k in GROUP_ENDS:
                    last.then_inc(sym_ps, 1)

            def accumulate(qs, k):
                hs = hs_of[qs[0] // NC]
                for part in range(2):
                    for q in qs:
                        c = q % NC
                        last = nc.tensor.matmul(bank[c][:, :], hs[:, k, part, :], adj8[:, k, c * CW:(c + 1) * CW],
                                                start=(k == 0 and part == 0), stop=(k == T - 1 and part == 1))
                        if k == T - 1 and part == 1:
                            last.then_inc(acc_done, 1)

            def back(q):
                pe.wait_ge(relu_ok, q + 1)
                for t in range(TC):
                    last = nc.tensor.transpose(bank[q % NC][:, t * P:(t + 1) * P], reluT[:, q % 2, t * P:(t + 1) * P],
                                               ident[:, :])
                last.then_inc(back_ps, 1)

            def transpose_n(q):
                pe.wait_ge(n_ok, q + 1)
                for t in range(TC):
                    last = nc.tensor.transpose(bank[q % NC][:, t * P:(t + 1) * P], nres[:, (q % NC) * TC + t, :],
                                               ident[:, :])
                last.then_inc(nT_ps, 1)

            def project(q):
                pe.wait_ge(nT_ok, q + 1)
                for t in range(TC):
                    last = nc.tensor.matmul(bank[q % NC][:, t * E:(t + 1) * E], nT[:, q % 2, t * P:(t + 1) * P],
                                            w_sb[:, q // NC + 1, :], start=True, stop=True)
                last.then_inc(h_ps, 1)

            pe.wait_ge(ident_ok, 1)
            transpose_x(0)
            pe.wait_ge(params_in, 16 * 4 * LAYERS)
            project_x(0)
            pe.wait_ge(const_ok, 1)
            for k in range(T):
                if k:
                    pe.wait_ge(lo1_ok, k)
                    accumulate(range(NA), k - 1)
                if k % TC == 1 and k // TC + 1 < NC:
                    transpose_x(k // TC + 1)
                symmetry(k)
                if k % TC == 1 and k // TC + 1 < NC:
                    project_x(k // TC + 1)
            pe.wait_ge(lo1_ok, T)
            accumulate(range(NA), T - 1)

            due = {}
            for q in range(NC):
                at = 3 + 11 * q
                for step, lag in ((back, 0), (transpose_n, 20), (project, 26)):
                    due.setdefault(at + lag, []).append((step, q))
            g = 0

            def advance(n):
                nonlocal g
                for _ in range(n):
                    for step, q in due.get(g, ()):
                        step(q)
                    g += 1

            for q in range(NA, NC):
                if q == PRO_BANK:
                    pe.wait_ge(h1_ok, NC)
                if q == SYM_BANK:
                    pe.wait_ge(sym_read, len(GROUPS))
                for k in range(T):
                    accumulate([q], k)
                    advance(1)
            for q in (NC, NC + 1):
                pe.wait_ge(h_ok, q - NC + 1)
            for k in range(T):
                if k % TC == 0:
                    pe.wait_ge(lo_ok, k // TC + 1)
                accumulate([NC, NC + 1], k)
                advance(2)
            assert max(due) < g

            for q in range(NC + 2, LAYERS * NC):
                l, c = divmod(q, NC)
                pe.wait_ge(h_ok, q - NC + 1)
                if q == LAYERS * NC - 1:
                    pe.wait_ge(clean_ok, 1)
                at = {4: [(back, q - 1)], 21: [(transpose_n, q - 1)], 25: [(project, q - 1)]}
                if q == NC + 2:
                    at = {3: [(back, NC)], 6: [(back, NC + 1)], 17: [(transpose_n, NC)], 21: [(project, NC)],
                          24: [(transpose_n, NC + 1)], 28: [(project, NC + 1)]}
                for k in range(T):
                    if c == 0 and k % TC == 0:
                        pe.wait_ge(lo_ok, (l - 1) * NC + k // TC + 1)
                    accumulate([q], k)
                    for step, e in at.get(k, ()):
                        if step is back or e < 2 * NC:
                            step(e)
                if q == 2 * NC + 1:
                    pe.wait_ge(ev_step, 2)
                    pe.wait_ge(h_ok, 2 * NC)
                    nc.tensor.matmul(bank[NC - 1][0:1, 0:1], ev_sum[:, :], ones[:, :], start=True,
                                     stop=True).then_inc(ev_ps, 1)
            back(LAYERS * NC - 1)
            with unless_clean(pe):
                general_tensor(nc, pe, m)


_PARAMS = ["W", "b", "g", "be"]


def kernel(**inputs):
    import numpy as _np
    import concourse.bacc as _bacc
    from concourse import mybir as _mybir
    from concourse.bass_utils import run_bass_kernel_spmd as _run

    nc = _bacc.Bacc("TRN2", target_bir_lowering=False, num_devices=1)
    arrays, aps = {}, {}
    for name in ["x", "adj"] + [f"L0_gnn_{p}{l + 1}" for p in _PARAMS for l in range(LAYERS)]:
        a = _np.ascontiguousarray(inputs[name])
        arrays[f"in_{name}"] = a
        aps[name] = nc.dram_tensor(f"in_{name}", a.shape, _mybir.dt.from_np(a.dtype), kind="ExternalInput").ap()
    out = nc.dram_tensor("out_0", (N, E), _mybir.dt.float32, kind="ExternalOutput").ap()
    w, b, g, be = ([aps[f"L0_gnn_{p}{l + 1}"] for l in range(LAYERS)] for p in _PARAMS)
    build(nc, aps["x"], aps["adj"], w, b, g, be, out)
    r = _run(nc, [arrays], core_ids=[0])
    return r.results[0]["out_0"]
```

```python
from contextlib import ExitStack

import concourse.bass as bass
from concourse import mybir

FP32 = mybir.dt.float32
FP16 = mybir.dt.float16
FP8 = mybir.dt.float8e4
I32 = mybir.dt.int32
ALU = mybir.AluOpType
ACT = mybir.ActivationFunctionType
AX = mybir.AxisListType

P = 128
N = 4096
E = 128
T = N // P
CW = 512
NC = N // CW
TC = CW // P
LAYERS = 3
EPS = 1e-5
HS_SCALE = 4096.0

UNIT = 2048
SLOTS = 4
UPPER = [(k, c, min(UNIT, N - c)) for k in range(T) for c in range(k * P, N, UNIT)]
UPPER_OF = [[u for u, (kk, _, _) in enumerate(UPPER) if kk == k] for k in range(T)]
LUNIT = 512
LSLOTS = 5
LOWER = [(k, c, min(LUNIT, k * P - c)) for k in range(T) for c in range(0, k * P, LUNIT)]
PARTS = 16
NA = 5
XPARTS = 4

SPARE = NC - NA
AHEAD = 4
ACT_HEAD, ACT_COL, ACT_ROW, DVE_COL, DVE_ROW = 0.0, 1.6e-3, 0.7, 1.8e-3, 1.8
WORK = {"act": ACT_HEAD, "dve": 0.0}
USES, USES_OF, LAST_MIRROR = [("xT", 0, 0, "act"), ("h1", 0, 0, "dve")], [], [None] * T
_left = [(k, j) for k in range(T) for j in range(0, k, TC)]
for _k in range(T):
    _first = len(USES)
    WORK["act"] += ACT_COL * (N - _k * P) + ACT_ROW
    WORK["dve"] += DVE_COL * (N - _k * P) + DVE_ROW
    if _k // TC + 1 < NC:
        if _k % TC == 1:
            USES.append(("xT", _k // TC + 1, 0, "act"))
        if _k % TC == 2:
            USES.append(("h1", _k // TC + 1, 0, "dve"))
    for _to, _j in list(_left):
        if _to == _k or (len(USES) - _first < AHEAD and _to < T - 5 and _j + TC <= min(_k, _to)):
            _left.remove((_to, _j))
            LAST_MIRROR[_to] = len(USES)
            _engine = min(WORK, key=WORK.get)
            WORK[_engine] += 1
            USES.append(("mirror", (_to, _j), min(TC, _to - _j), _engine))
    USES_OF.append(list(range(_first, len(USES))))


BEHIND = 2
AT_ONCE = 2
SCALED = 1

def reads(engine, use):
    return sum(u[3] == engine for u in USES[:use + 1])


ITEMS = [(l, c, c * TC, TC) for l in range(LAYERS) for c in range(NC)]
_l, _c, _t, _n = ITEMS.pop()
ITEMS += [(_l, _c, _t, _n // 2), (_l, _c - 2, _t + _n // 2, _n // 2)]
LAST = 2 * NC
PACE, G_LAG, N_LAG, H_LAG, VERIFY = 12, 14, 27, 31, 2
WIDE = 4

FIRST_AT = [0] * NA + [(q - NA + 1) * T for q in range(NA, NC)]
FIRST_AT += [(NC - NA + max(WIDE, q - NC + 1)) * T for q in range(NC, LAST)]
FIRST_AT += [FIRST_AT[-1] + max(2, q - LAST + 1) * T for q in range(LAST, len(ITEMS))]
BACK_AT = []
for _q, _f in enumerate(FIRST_AT):
    _at = max(_f + 3, BACK_AT[-1] + (PACE if _q < LAST else 4) if BACK_AT else 0)
    BACK_AT.append(_at)
SUM_AT = BACK_AT[-2] + 18

EV_UPPER = 0
EV_LOWER = EV_UPPER + len(UPPER)
EV_DIAG = EV_LOWER + len(LOWER)
EV_LO = EV_DIAG + NC
EV_END = EV_LO + LAYERS * T


_NORM = ["y", "stats", "moments", "variance", "rstd", "centred"]
_NEXT = ["n_transposed", "nT_copied", "projected", "h", "h_kept", "h_scaled", "hs_stored"]
_LAYER = ["row_transposed", "rowT_copied", "summed", "dinv_fetched", "residual_fetched", "scaled"]
STEPS = ([["row_summed", "dinv_found", "dinv_kept"] + _NORM + ["n"] + _NEXT]
         + [_LAYER + _NORM + ["gained", "n"] + _NEXT] * (LAYERS - 1)
         + [_LAYER + _NORM + ["gained", "n", "result"]])


def tile_begins(stage, i):
    return i * len(STEPS[stage]) + (1 + T * sum(len(STEPS[s]) for s in range(stage)))


def after(stage, i, step):
    return tile_begins(stage, i) + (STEPS[stage].index(step) + 1)


def general_sync(nc, sp, m):
    for stage in range(LAYERS + 1):
        with sp.Fori(0, T) as i:
            sp.wait_ge(m.step, tile_begins(stage, i))
            sp.dma_start(m.row[:, :], m.adj[bass.ts(i, P), :]).then_inc(m.row_in, 16)
            if stage in (0, LAYERS):
                sp.dma_start(m.xt[:, :], m.x[bass.ts(i, P), :]).then_inc(m.x_in, 16)
            if stage == LAYERS:
                sp.wait_ge(m.step, after(stage, i, "result"))
                sp.dma_start(m.out[bass.ts(i, P), :], m.result[:, :]).then_inc(m.stored, 16)
    sp.wait_ge(m.stored, 16 * T)


def general_tensor(nc, pe, m):
    for stage in range(LAYERS + 1):
        with pe.Fori(0, T) as i:
            if stage:
                pe.wait_ge(m.row_in, (i + (stage * T + 1)) * 16)
                for k in range(T):
                    last = nc.tensor.transpose(m.bank[k // TC][:, (k % TC) * P:(k % TC + 1) * P],
                                               m.row[:, k * P:(k + 1) * P], m.ident[:, :])
                last.then_inc(m.step, 1)
                pe.wait_ge(m.step, after(stage, i, "rowT_copied"))
                for k in range(T):
                    last = nc.tensor.matmul(m.bank[0][:, 0:E], m.rowT[:, k, :], m.hs[(stage - 1) % 2][:, k, :],
                                            start=(k == 0), stop=(k == T - 1))
                last.then_inc(m.step, 1)
            if stage < LAYERS:
                pe.wait_ge(m.step, after(stage, i, "n"))
                nc.tensor.transpose(m.bank[1][:, 0:P], m.n[:, :], m.ident[:, :]).then_inc(m.step, 1)
                pe.wait_ge(m.step, after(stage, i, "nT_copied"))
                nc.tensor.matmul(m.bank[2][:, 0:E], m.nT[:, :], m.w[:, stage, :], start=True,
                                 stop=True).then_inc(m.step, 1)


def general_scalar(nc, act, m):
    for stage in range(LAYERS + 1):
        with act.Fori(0, T) as i:
            if stage:
                act.wait_ge(m.step, after(stage, i, "row_transposed"))
                for c in range(NC):
                    last = nc.scalar.activation(m.rowT[:, c * TC:(c + 1) * TC, :], m.tiles(m.bank[c][:, :]), ACT.Copy)
                last.then_inc(m.step, 1)
            if stage < LAYERS:
                act.wait_ge(m.step, after(stage, i, "n_transposed"))
                nc.scalar.activation(m.nT[:, :], m.bank[1][:, 0:P], ACT.Copy).then_inc(m.step, 1)


def general_pool(nc, pool, m):
    for stage in range(LAYERS + 1):
        with pool.Fori(0, T) as i:
            if stage == 0:
                pool.wait_ge(m.step, after(stage, i, "row_summed"))
                nc.gpsimd.tensor_tensor(m.dinv_i[:, :], m.rowsum_i[:, :], m.mhalf[:, 0:1], ALU.pow).then_inc(m.step, 1)
            pool.wait_ge(m.step, after(stage, i, "moments"))
            nc.gpsimd.tensor_tensor(m.var[:, :], m.mv[:, 1:2], m.eps[:, :], ALU.add).then_inc(m.step, 1)
            pool.wait_ge(m.step, after(stage, i, "variance"))
            nc.gpsimd.tensor_tensor(m.rstd[:, :], m.var[:, :], m.mhalf[:, 0:1], ALU.pow).then_inc(m.step, 1)


def general_vector(nc, dve, m):
    def carry():
        nc.vector.memset(m.carrier[:, :], 0.0)

    nc.vector.memset(m.eps[:, :], EPS).then_inc(m.step, 1)
    for stage in range(LAYERS + 1):
        with dve.Fori(0, T) as i:
            def then(ins, step):
                ins.then_inc(m.step, 1)
                dve.wait_ge(m.step, after(stage, i, step))

            if stage:
                dve.wait_ge(m.step, after(stage, i, "summed"))
                carry()
                then(nc.vector.tensor_copy(m.dinv_i[:, :], m.dinv[:, bass.ds(i, 1)]), "dinv_fetched")
                carry()
                then(nc.vector.tensor_copy(m.res_i[:, :], m.res[:, bass.ds(i, 1), :]), "residual_fetched")
                then(nc.vector.tensor_scalar(m.y[:, :], m.bank[0][:, 0:E], m.dinv_i[:, :], 0.0, ALU.mult, ALU.max),
                     "scaled")
                then(nc.vector.tensor_tensor(m.y[:, :], m.y[:, :], m.res_i[:, :], ALU.add), "y")
            else:
                dve.wait_ge(m.x_in, (i + 1) * 16)
                dve.wait_ge(m.row_in, (i + 1) * 16)
                dve.wait_ge(m.step, tile_begins(stage, i))
                then(nc.vector.tensor_reduce(m.rowsum_i[:, :], m.row[:, :], AX.X, ALU.add), "row_summed")
                dve.wait_ge(m.step, after(stage, i, "dinv_found"))
                carry()
                then(nc.vector.tensor_copy(m.dinv[:, bass.ds(i, 1)], m.dinv_i[:, :]), "dinv_kept")
                then(nc.vector.tensor_copy(m.y[:, :], m.xt[:, :]), "y")
            then(nc.vector.bn_stats(m.st[:, :], m.y[:, :]), "stats")
            carry()
            then(nc.vector.bn_aggr(m.mv[:, :], m.st[:, :]), "moments")
            dve.wait_ge(m.step, after(stage, i, "rstd"))
            then(nc.vector.tensor_scalar(m.y[:, :], m.y[:, :], m.mv[:, 0:1], m.rstd[:, :], ALU.subtract, ALU.mult),
                 "centred")
            if stage:
                then(nc.vector.tensor_tensor(m.y[:, :], m.y[:, :], m.g[:, stage - 1, :], ALU.mult), "gained")
                then(nc.vector.tensor_tensor(m.n[:, :], m.y[:, :], m.be[:, stage - 1, :], ALU.add), "n")
            else:
                then(nc.vector.tensor_scalar(m.n[:, :], m.y[:, :], 0.0, None, ALU.max), "n")
            if stage < LAYERS:
                dve.wait_ge(m.step, after(stage, i, "projected"))
                then(nc.vector.tensor_tensor(m.h[:, :], m.bank[2][:, 0:E], m.b[:, stage, :], ALU.add), "h")
                kept = m.n if stage else m.h
                carry()
                then(nc.vector.tensor_copy(m.res[:, bass.ds(i, 1), :], kept[:, :]), "h_kept")
                then(nc.vector.tensor_scalar(m.h[:, :], m.h[:, :], m.dinv_i[:, :], None, ALU.mult), "h_scaled")
                carry()
                then(nc.vector.tensor_copy(m.hs[stage % 2][:, bass.ds(i, 1), :], m.h[:, :]), "hs_stored")
            else:
                dve.wait_ge(m.x_in, (i + T + 1) * 16)
                then(nc.vector.tensor_tensor(m.result[:, :], m.n[:, :], m.xt[:, :], ALU.add), "result")


def build(nc, x, adj, w, b, g, be, out):
    x_v = x.rearrange("(t p) e -> p t e", p=P)
    out_v = out.rearrange("(t p) e -> p t e", p=P)
    adj_v = adj.rearrange("(t p) n -> t p n", p=P)

    ctx = ExitStack()
    with ctx:
        def sb(name, shape, dt):
            return ctx.enter_context(nc.sbuf_tensor(name, shape, dt))

        def sem(name):
            return ctx.enter_context(nc.semaphore(name))

        adj8 = sb("adj8", [P, T, N], FP8)
        room = sb("room", [P, SLOTS * UNIT + UNIT // 2], FP32)
        nres = sb("nres", [P, T, E], FP32)
        hs_a = sb("hs_a", [P, T, 2, E], FP16)
        ident = sb("ident", [P, P], FP32)
        ident8 = sb("ident8", [P, P], FP8)
        w_sb = sb("w_sb", [P, LAYERS, E], FP32)
        b_bc = sb("b_bc", [P, LAYERS, E], FP32)
        g_bc = sb("g_bc", [P, LAYERS, E], FP32)
        be_bc = sb("be_bc", [P, LAYERS, E], FP32)
        evidence = sb("evidence", [P, EV_END], FP32)
        rs_part = sb("rs_part", [P, T, PARTS], FP32)
        rowsum = sb("rowsum", [P, T], FP32)
        dinv = sb("dinv", [P, T], FP32)
        dinv_in = sb("dinv_in", [P, T], FP32)
        dinv_out = sb("dinv_out", [P, T], FP32)
        mhalf = sb("mhalf", [P, TC], FP32)
        ones = sb("ones", [P, 1], FP32)
        st0 = sb("st0", [P, TC, 6], FP32)
        mv0 = sb("mv0", [P, TC, 2], FP32)
        var0 = sb("var0", [P, TC], FP32)
        rstd0 = sb("rstd0", [P, T], FP32)
        st = sb("st", [P, TC, 6], FP32)
        mv = sb("mv", [P, 2, TC, 2], FP32)
        vare = sb("vare", [P, 2, TC], FP32)
        rstd = sb("rstd", [P, 2, TC], FP32)
        nmean = sb("nmean", [P, 2, TC], FP32)
        nmr = sb("nmr", [P, 2, TC], FP32)
        ev_sum = sb("ev_sum", [P, 1], FP32)
        tick = sb("tick", [P, 1], FP32)
        clean = sb("clean", [1, 1], I32)

        x_sb = adj8[:, T - 4:T, :].rearrange("p a n -> p (a n)").bitcast(FP32).rearrange("p (t e) -> p t e", e=E)
        xT = adj8[:, T - 5:T - 4, :].rearrange("p a n -> p (a n)").bitcast(FP32).rearrange("p (s n) -> p s n", n=CW)
        stage = room[:, 0:SLOTS * UNIT].rearrange("p (s n) -> p s n", n=UNIT)
        junk = room[:, SLOTS * UNIT:].bitcast(FP8).rearrange("p (s n) -> p s n", n=UNIT)
        hs_b = room[:, 0:N].bitcast(FP16).rearrange("p (t h e) -> p t h e", h=2, e=E)
        xb = room[:, 0:N].rearrange("p (t e) -> p t e", e=E)

        def tiles_of(t):
            return t[:, :].rearrange("p (t e) -> p t e", e=E)

        def slots(first, n, width):
            return room[:, first:first + n * width].rearrange("p (s n) -> p s n", n=width)

        reluT = slots(N, 2, CW)
        yb = slots(N + 2 * CW, 2, CW)
        nT = slots(N + 4 * CW, 1, CW)
        hb = slots(N + 5 * CW, 1, CW)
        lstage = slots(N + 6 * CW, LSLOTS - 1, LUNIT)
        lslot = [lstage[:, i, :] for i in range(LSLOTS - 1)] + [rs_part[:, :, :].rearrange("p t n -> p (t n)")]
        diag_out = tiles_of(sb("diag_out", [P, CW], FP8))
        hs_of = [hs_a, hs_b, hs_a]

        bank = [ctx.enter_context(nc.psum_tensor(f"bank{i}", [P, CW], FP32)) for i in range(NC)]

        def tiles(ap):
            return ap.rearrange("p (t e) -> p t e", e=E)

        x_in = [sem(f"x_in{i}") for i in range(XPARTS)]
        first_in = sem("first_in")
        params_in = sem("params_in")
        x_again = sem("x_again")
        slot_in = [sem(f"slot_in{i}") for i in range(SLOTS)]
        ident_0 = sem("ident_0")
        ident_ok = sem("ident_ok")
        const_ok = sem("const_ok")
        converted = sem("converted")
        checked = sem("checked")
        lslot_in = [sem(f"lslot_in{i}") for i in range(LSLOTS)]
        verified = sem("verified")
        spare_filled = sem("spare_filled")
        read_by = {"act": sem("spare_read_act"), "dve": sem("spare_read_dve")}
        parts_zero = sem("parts_zero")
        diag_ps = sem("diag_ps")
        diag_ok = sem("diag_ok")
        pool_step = sem("pool_step")
        dinv_ok = sem("dinv_ok")
        dout_ok = sem("dout_ok")
        stat0 = sem("stat0")
        mv0_ok = sem("mv0_ok")
        rstd0_ok = sem("rstd0_ok")
        relu0_ok = sem("relu0_ok")
        xT_ok = sem("xT_ok")
        h1_ok = sem("h1_ok")
        hi1_ok = sem("hi1_ok")
        lo1_ok = sem("lo1_ok")
        acc_done = sem("acc_done")
        relu_ok = sem("relu_ok")
        back_ps = sem("back_ps")
        y_ok = sem("y_ok")
        stat_ok = sem("stat_ok")
        mv_ok = sem("mv_ok")
        rstd_ok = sem("rstd_ok")
        nmean_ok = sem("nmean_ok")
        z_ok = sem("z_ok")
        zg_ok = sem("zg_ok")
        n_ok = sem("n_ok")
        nT_ps = sem("nT_ps")
        nT_ok = sem("nT_ok")
        h_ps = sem("h_ps")
        h_ok = sem("h_ok")
        hi_ok = sem("hi_ok")
        lo_ok = sem("lo_ok")
        xb_ok = sem("xb_ok")
        ev_step = sem("ev_step")
        ev_ps = sem("ev_ps")
        clean_ok = sem("clean_ok")
        out_done = sem("out_done")

        class General:
            pass

        m = General()
        taken = [0]

        def place(cols):
            first = taken[0]
            taken[0] += cols
            return adj8[:, :, :].rearrange("p t n -> p (t n)").bitcast(FP32)[:, first:taken[0]]

        m.x, m.adj, m.out = x, adj, out
        m.row = place(N)
        m.rowT = place(N).rearrange("p (t n) -> p t n", n=P)
        m.hs = [place(N).rearrange("p (t n) -> p t n", n=E) for _ in range(2)]
        m.xt, m.y, m.res_i, m.n, m.nT, m.h, m.result = (place(E) for _ in range(7))
        m.dinv_i, m.rowsum_i, m.var, m.rstd, m.eps, m.carrier = (place(1) for _ in range(6))
        m.st, m.mv = place(6), place(2)
        m.res, m.dinv, m.ident, m.mhalf = nres, dinv, ident, mhalf
        m.w, m.b, m.g, m.be, m.bank, m.tiles = w_sb, b_bc, g_bc, be_bc, bank, tiles
        m.step = sem("general_step")
        m.row_in = sem("general_row_in")
        m.x_in = sem("general_x_in")
        m.stored = sem("general_stored")

        def unless_clean(eng):
            eng.wait_ge(clean_ok, 1)
            verdict = eng.alloc_register()
            eng.reg_load(verdict, clean[0:1, 0:1])
            return eng.If_eq(verdict, 0)

        block = ctx.enter_context(nc.Block())

        @block.sync
        def _(sp):
            for u, (k, c0, width) in enumerate(UPPER):
                if u >= SLOTS:
                    sp.wait_ge(converted, u - SLOTS + 1)
                    sp.wait_ge(checked, u - SLOTS + 1)
                sp.dma_start(stage[:, u % SLOTS, 0:width],
                             adj_v[k, :, c0:c0 + width]).then_inc(slot_in[u % SLOTS], 16)
            for v, (k, c0, width) in enumerate(LOWER):
                if v == LSLOTS - 1:
                    sp.wait_ge(dout_ok, 1)
                if v == 0:
                    sp.wait_ge(converted, len(UPPER))
                    sp.wait_ge(checked, len(UPPER))
                if v >= LSLOTS:
                    sp.wait_ge(verified, v - LSLOTS + 1)
                sp.dma_start(lslot[v % LSLOTS][:, 0:width],
                             adj_v[k, :, c0:c0 + width]).then_inc(lslot_in[v % LSLOTS], 16)
            for q in range(LAST, len(ITEMS)):
                _, _, t0, nt = ITEMS[q]
                sp.wait_ge(n_ok, q + 1)
                sp.dma_start(out_v[:, t0:t0 + nt, :], nres[:, t0:t0 + nt, :]).then_inc(out_done, 16)
            sp.wait_ge(out_done, 16 * (len(ITEMS) - LAST))
            with unless_clean(sp):
                general_sync(nc, sp, m)

        @block.gpsimd
        def _(pool):
            steps = [0]

            def chain(ins):
                steps[0] += 1
                ins.then_inc(pool_step, 1)
                pool.wait_ge(pool_step, steps[0])

            nc.gpsimd.memset(ident[:, :], 0.0).then_inc(ident_0, 1)
            nc.gpsimd.memset(mhalf[:, :], -0.5)
            nc.gpsimd.memset(rs_part[:, :, :], 0.0).then_inc(parts_zero, 1)
            nc.gpsimd.memset(ones[:, :], 1.0)
            pool.wait_ge(ident_0, 1)
            nc.gpsimd.affine_select(out=ident[:, :], in_=ident[:, :], compare_op=ALU.not_equal, fill=1.0,
                                    base=0, pattern=[[-1, P]], channel_multiplier=1).then_inc(ident_ok, 1)
            pool.wait_ge(ident_ok, 1)

            def rstd_of_x(i):
                pool.wait_ge(mv0_ok, i + 1)
                chain(nc.gpsimd.tensor_scalar(var0[:, :], mv0[:, :, 1], EPS, None, ALU.add))
                nc.gpsimd.tensor_tensor(rstd0[:, i * TC:(i + 1) * TC], var0[:, :], mhalf[:, :],
                                        ALU.pow).then_inc(rstd0_ok, 1)

            rstd_of_x(0)
            for k in range(T):
                if k % TC == 0 and k // TC + 1 < NC:
                    rstd_of_x(k // TC + 1)
                pool.wait_ge(converted, UPPER_OF[k][-1] + 1)
                if k:
                    for engine in ("act", "dve"):
                        if reads(engine, LAST_MIRROR[k]):
                            pool.wait_ge(read_by[engine], reads(engine, LAST_MIRROR[k]))
                width = PARTS // 2
                while width > 1:
                    chain(nc.gpsimd.tensor_tensor(rs_part[:, k, 0:width], rs_part[:, k, 0:width],
                                                  rs_part[:, k, width:2 * width], ALU.add))
                    width //= 2
                chain(nc.gpsimd.tensor_tensor(rowsum[:, k:k + 1], rs_part[:, k, 0:1], rs_part[:, k, 1:2], ALU.add))
                chain(nc.gpsimd.tensor_tensor(dinv[:, k:k + 1], rowsum[:, k:k + 1], mhalf[:, 0:1], ALU.pow))
                nc.gpsimd.tensor_scalar(dinv_in[:, k:k + 1], dinv[:, k:k + 1], HS_SCALE, None,
                                        ALU.mult).then_inc(dinv_ok, 1)
            nc.gpsimd.tensor_scalar(dinv_out[:, :], dinv[:, :], 1.0 / HS_SCALE, None, ALU.mult).then_inc(dout_ok, 1)

            def shift(q):
                l, _, t0, nt = ITEMS[q]
                pool.wait_ge(zg_ok, q + 1)
                nc.gpsimd.tensor_tensor(nres[:, t0:t0 + nt, :], tiles(yb[:, q % 2, :])[:, 0:nt, :],
                                        be_bc[:, l:l + 1, :].to_broadcast([P, nt, E]), ALU.add).then_inc(n_ok, 1)

            for q in range(len(ITEMS)):
                l, _, _, nt = ITEMS[q]
                if q == LAST:
                    pool.wait_ge(acc_done, LAST)
                    pool.dma_start(xb, x_v).then_inc(x_again, 16)
                    pool.wait_ge(x_again, 16)
                    nc.gpsimd.tensor_tensor(xb, xb, be_bc[:, LAYERS - 1:LAYERS, :].to_broadcast([P, T, E]),
                                            ALU.add).then_inc(xb_ok, 1)
                pool.wait_ge(mv_ok, q + 1)
                if q >= 2:
                    pool.wait_ge(z_ok, q - 1)
                chain(nc.gpsimd.tensor_scalar(vare[:, q % 2, 0:nt], mv[:, q % 2, 0:nt, 1], EPS, None, ALU.add))
                last = nc.gpsimd.tensor_tensor(rstd[:, q % 2, 0:nt], vare[:, q % 2, 0:nt], mhalf[:, 0:nt], ALU.pow)
                if q < LAST:
                    chain(last)
                    pool.wait_ge(nmean_ok, q + 1)
                    last = nc.gpsimd.tensor_tensor(nmr[:, q % 2, :], nmean[:, q % 2, :], rstd[:, q % 2, :], ALU.mult)
                last.then_inc(rstd_ok, 1)
                if q < LAST:
                    shift(q)
            with unless_clean(pool):
                general_pool(nc, pool, m)

        @block.scalar
        def _(act):
            tx = T // XPARTS
            for i in range(XPARTS):
                act.dma_start(x_sb[:, i * tx:(i + 1) * tx, :], x_v[:, i * tx:(i + 1) * tx, :]).then_inc(x_in[i], 16)
                if i == 0:
                    act.dma_start(w_sb[:, 0, :], w[0]).then_inc(first_in, 16)
                    act.dma_start(b_bc[:, 0, :], b[0].partition_broadcast(P)).then_inc(first_in, 16)
            for l in range(LAYERS):
                if l:
                    act.dma_start(w_sb[:, l, :], w[l]).then_inc(params_in, 16)
                    act.dma_start(b_bc[:, l, :], b[l].partition_broadcast(P)).then_inc(params_in, 16)
                act.dma_start(g_bc[:, l, :], g[l].partition_broadcast(P)).then_inc(params_in, 16)
                act.dma_start(be_bc[:, l, :], be[l].partition_broadcast(P)).then_inc(params_in, 16)

            def convert(u):
                k, c0, width = UPPER[u]
                act.wait_ge(slot_in[u % SLOTS], 16 * (u // SLOTS + 1))
                nc.scalar.activation(adj8[:, k, c0:c0 + width], stage[:, u % SLOTS, 0:width], ACT.Copy,
                                     accum_out=rs_part[:, k, u - UPPER_OF[k][0]:u - UPPER_OF[k][0] + 1],
                                     saturate=False).then_inc(converted, 1)

            def read_spare(use, k):
                kind, i, n, engine = USES[use]
                if engine != "act":
                    return
                act.wait_ge(spare_filled, use + 1)
                src = bank[NA + use % SPARE]
                if kind == "xT":
                    if i >= 2:
                        act.wait_ge(h1_ok, i - 1)
                    nc.scalar.activation(xT[:, i % 2, :], src[:, :], ACT.Copy).then_inc(read_by["act"], 1)
                else:
                    k, i = i
                    nc.scalar.activation(adj8[:, k, i * P:(i + n) * P], src[:, 0:n * P], ACT.Copy,
                                         accum_out=rs_part[:, k, 2 + i // TC:3 + i // TC],
                                         saturate=False).then_inc(read_by["act"], 1)

            def high_1(k):
                act.wait_ge(dinv_ok, k + 1)
                act.wait_ge(h1_ok, k // TC + 1)
                nc.scalar.activation(hs_a[:, k, 0, :], nres[:, k, :], ACT.Copy,
                                     scale=dinv_in[:, k:k + 1]).then_inc(hi1_ok, 1)

            act.wait_ge(parts_zero, 1)
            read_spare(0, 0)
            for k in range(T):
                if k == T - 5:
                    act.wait_ge(h1_ok, NC)
                uses, units = USES_OF[k], UPPER_OF[k]
                half = (len(uses) + 1) // 2
                convert(units[0])
                for use in uses[:half]:
                    read_spare(use, k)
                if k >= SCALED:
                    high_1(k - SCALED)
                for u in units[1:]:
                    convert(u)
                for use in uses[half:]:
                    read_spare(use, k)
            for k in range(T - SCALED, T):
                high_1(k)

            def relu_out(q):
                _, bk, _, nt = ITEMS[q]
                act.wait_ge(acc_done, q + 1)
                if q == 0:
                    act.wait_ge(checked, len(UPPER))
                if q >= 2:
                    act.wait_ge(back_ps, q - 1)
                nc.scalar.activation(reluT[:, q % 2, 0:nt * P], bank[bk][:, 0:nt * P], ACT.Relu).then_inc(relu_ok, 1)

            def standardise(q):
                act.wait_ge(rstd_ok, q + 1)
                y = tiles(yb[:, q % 2, :])
                for t in range(TC):
                    last = nc.scalar.activation(y[:, t, :], y[:, t, :], ACT.Identity, bias=nmr[:, q % 2, t:t + 1],
                                                scale=rstd[:, q % 2, t:t + 1])
                last.then_inc(z_ok, 1)

            def copy_nT(q):
                act.wait_ge(nT_ps, q + 1)
                if q:
                    act.wait_ge(h_ps, q)
                nc.scalar.activation(nT[:, 0, :], bank[ITEMS[q][1]][:, :], ACT.Copy).then_inc(nT_ok, 1)

            def high(q):
                l, _, t0, nt = ITEMS[q]
                act.wait_ge(h_ok, q + 1)
                for t in range(nt):
                    k = t0 + t
                    last = nc.scalar.activation(hs_of[l + 1][:, k, 0, :], tiles(hb[:, 0, :])[:, t, :], ACT.Copy,
                                                scale=dinv_in[:, k:k + 1])
                last.then_inc(hi_ok, 1)

            order = []
            for q in range(LAST):
                order.append((max(FIRST_AT[q], BACK_AT[q] - 10), relu_out, q))
                order.append((BACK_AT[q] + 12, standardise, q))
                order.append((BACK_AT[q] + N_LAG, copy_nT, q))
                order.append((BACK_AT[q] + H_LAG + 2, high, q))
            for _, step, q in sorted(order, key=lambda entry: entry[0]):
                step(q)
            for q in range(LAST, len(ITEMS)):
                relu_out(q)
            with unless_clean(act):
                general_scalar(nc, act, m)

        @block.vector
        def _(dve):
            def check(u):
                _, _, width = UPPER[u]
                dve.wait_ge(slot_in[u % SLOTS], 16 * (u // SLOTS + 1))
                if u >= 2:
                    dve.wait_ge(checked, u - 1)
                src = stage[:, u % SLOTS, 0:width]
                nc.vector.scalar_tensor_tensor(out=junk[:, u % 2, 0:width], in0=src, scalar=1.0, in1=src,
                                               op0=ALU.is_equal, op1=ALU.not_equal,
                                               accum_out=evidence[:, EV_UPPER + u:EV_UPPER + u + 1],
                                               saturate=False).then_inc(checked, 1)

            def verify(v):
                k, c0, width = LOWER[v]
                dve.wait_ge(lslot_in[v % LSLOTS], 16 * (v // LSLOTS + 1))
                src = lslot[v % LSLOTS][:, 0:width]
                nc.vector.scalar_tensor_tensor(out=src, in0=src, scalar=1.0, in1=adj8[:, k, c0:c0 + width],
                                               op0=ALU.mult, op1=ALU.not_equal,
                                               accum_out=evidence[:, EV_LOWER + v:EV_LOWER + v + 1]
                                               ).then_inc(verified, 1)

            def verify_diagonal(d):
                dve.wait_ge(diag_ps, d + 1)
                if d:
                    dve.wait_ge(diag_ok, d)
                first = d * TC * (T + 1)
                own = adj8[:, :, :].rearrange("p t (s n) -> p (t s) n", n=P)[:, first:first + (TC - 1) * (T + 1) + 1:T + 1, :]
                nc.vector.scalar_tensor_tensor(out=diag_out, in0=tiles(bank[NC - 2 + d % 2][:, :]), scalar=1.0, in1=own,
                                               op0=ALU.mult, op1=ALU.not_equal,
                                               accum_out=evidence[:, EV_DIAG + d:EV_DIAG + d + 1],
                                               saturate=False).then_inc(diag_ok, 1)

            def norm_x(i):
                if i % (NC // XPARTS) == 0:
                    dve.wait_ge(x_in[i // (NC // XPARTS)], 16)
                for t in range(TC):
                    last = nc.vector.bn_stats(st0[:, t, :], x_sb[:, i * TC + t, :])
                last.then_inc(stat0, 1)
                dve.wait_ge(stat0, i + 1)
                if i:
                    dve.wait_ge(rstd0_ok, i)
                for t in range(TC):
                    last = nc.vector.bn_aggr(mv0[:, t, :], st0[:, t, :])
                last.then_inc(mv0_ok, 1)
                dve.wait_ge(mv0_ok, i + 1)
                for t in range(TC):
                    xt = x_sb[:, i * TC + t, :]
                    last = nc.vector.tensor_scalar(xt, xt, mv0[:, t, 0:1], 0.0, ALU.subtract, ALU.max)
                last.then_inc(relu0_ok, 1)

            def h_1(i, src):
                dve.wait_ge(rstd0_ok, i + 1)
                for t in range(TC):
                    k = i * TC + t
                    last = nc.vector.scalar_tensor_tensor(out=nres[:, k, :], in0=tiles(src)[:, t, :],
                                                          scalar=rstd0[:, k:k + 1], in1=b_bc[:, 0, :],
                                                          op0=ALU.mult, op1=ALU.add)
                last.then_inc(h1_ok, 1)

            def read_spare(use, k):
                kind, i, n, engine = USES[use]
                if engine != "dve":
                    return
                dve.wait_ge(spare_filled, use + 1)
                src = bank[NA + use % SPARE]
                if kind == "h1":
                    h_1(i, src[:, :])
                    dve.wait_ge(h1_ok, i + 1)
                    nc.vector.memset(tick[:, :], 0.0).then_inc(read_by["dve"], 1)
                else:
                    k, i = i
                    nc.vector.tensor_scalar(adj8[:, k, i * P:(i + n) * P], src[:, 0:n * P], 0.0, 0.0, ALU.add, ALU.add,
                                            accum_out=rs_part[:, k, 2 + i // TC:3 + i // TC],
                                            saturate=False).then_inc(read_by["dve"], 1)

            def low_1(k):
                dve.wait_ge(hi1_ok, k + 1)
                nc.vector.scalar_tensor_tensor(out=hs_a[:, k, 1, :], in0=nres[:, k, :], scalar=dinv_in[:, k:k + 1],
                                               in1=hs_a[:, k, 0, :], op0=ALU.mult, op1=ALU.subtract,
                                               accum_out=evidence[:, EV_LO + k:EV_LO + k + 1]).then_inc(lo1_ok, 1)

            dve.wait_ge(ident_ok, 1)
            nc.vector.tensor_copy(ident8[:, :], ident[:, :], saturate=False).then_inc(const_ok, 1)
            dve.wait_ge(parts_zero, 1)
            norm_x(0)
            for k in range(T):
                if k == T - 5:
                    dve.wait_ge(read_by["act"], reads("act", USES_OF[k][0] - 1))
                uses, units = USES_OF[k], UPPER_OF[k]
                half = (len(uses) + 1) // 2
                check(units[0])
                for use in uses[:half]:
                    read_spare(use, k)
                if k >= SCALED:
                    low_1(k - SCALED)
                for u in units[1:]:
                    check(u)
                for use in uses[half:]:
                    read_spare(use, k)
                if k == 0:
                    norm_x(1)
                    dve.wait_ge(first_in, 32)
                    read_spare(1, 0)
                if k % TC == TC - 1 and k // TC + 2 < NC:
                    norm_x(k // TC + 2)
            for k in range(T - SCALED, T):
                low_1(k)
            dve.wait_ge(dout_ok, 1)
            dve.wait_ge(params_in, 16 * (4 * LAYERS - 2))

            def residual(q):
                l, bk, t0, nt = ITEMS[q]
                dve.wait_ge(back_ps, q + 1)
                if 2 <= q < LAST:
                    dve.wait_ge(n_ok, q - 1)
                y = tiles(yb[:, q % 2, :])
                for t in range(nt):
                    k = t0 + t
                    last = nc.vector.scalar_tensor_tensor(out=y[:, t, :], in0=tiles(bank[bk][:, :])[:, t, :],
                                                          scalar=dinv_out[:, k:k + 1], in1=nres[:, k, :],
                                                          op0=ALU.mult, op1=ALU.add)
                last.then_inc(y_ok, 1)
                dve.wait_ge(y_ok, q + 1)
                for t in range(nt):
                    last = nc.vector.bn_stats(st[:, t, :], y[:, t, :])
                last.then_inc(stat_ok, 1)
                dve.wait_ge(stat_ok, q + 1)
                if q >= 2:
                    dve.wait_ge(rstd_ok, q - 1)
                for t in range(nt):
                    last = nc.vector.bn_aggr(mv[:, q % 2, t, :], st[:, t, :])
                last.then_inc(mv_ok, 1)
                if q < LAST:
                    dve.wait_ge(mv_ok, q + 1)
                    nc.vector.tensor_scalar(nmean[:, q % 2, :], mv[:, q % 2, :, 0], -1.0, None,
                                            ALU.mult).then_inc(nmean_ok, 1)

            def gain(q):
                l, _, _, nt = ITEMS[q]
                y = tiles(yb[:, q % 2, :])[:, 0:nt, :]
                dve.wait_ge(z_ok, q + 1)
                nc.vector.tensor_tensor(y, y, g_bc[:, l:l + 1, :].to_broadcast([P, nt, E]), ALU.mult).then_inc(zg_ok, 1)

            def result(q):
                _, _, t0, nt = ITEMS[q]
                y = tiles(yb[:, q % 2, :])
                dve.wait_ge(rstd_ok, q + 1)
                for t in range(nt):
                    last = nc.vector.tensor_scalar(y[:, t, :], y[:, t, :], mv[:, q % 2, t, 0:1],
                                                   rstd[:, q % 2, t:t + 1], ALU.subtract, ALU.mult)
                last.then_inc(z_ok, 1)
                gain(q)
                dve.wait_ge(zg_ok, q + 1)
                dve.wait_ge(xb_ok, 1)
                nc.vector.tensor_tensor(nres[:, t0:t0 + nt, :], y[:, 0:nt, :], xb[:, t0:t0 + nt, :],
                                        ALU.add).then_inc(n_ok, 1)

            def bias(q):
                l, bk, _, nt = ITEMS[q]
                dve.wait_ge(h_ps, q + 1)
                if q:
                    dve.wait_ge(lo_ok, q)
                nc.vector.tensor_tensor(tiles(hb[:, 0, :]), tiles(bank[bk][:, :]),
                                        b_bc[:, l + 1:l + 2, :].to_broadcast([P, nt, E]), ALU.add).then_inc(h_ok, 1)

            def low(q):
                l, _, t0, nt = ITEMS[q]
                hs = hs_of[l + 1]
                dve.wait_ge(h_ok, q + 1)
                dve.wait_ge(hi_ok, q + 1)
                for t in range(nt):
                    k = t0 + t
                    ev = EV_LO + (l + 1) * T + k
                    last = nc.vector.scalar_tensor_tensor(out=hs[:, k, 1, :], in0=tiles(hb[:, 0, :])[:, t, :],
                                                          scalar=dinv_in[:, k:k + 1], in1=hs[:, k, 0, :],
                                                          op0=ALU.mult, op1=ALU.subtract,
                                                          accum_out=evidence[:, ev:ev + 1])
                last.then_inc(lo_ok, 1)

            def sum_up(_):
                dve.wait_ge(verified, len(LOWER))
                dve.wait_ge(lo_ok, LAST)
                dve.wait_ge(diag_ok, NC)
                nc.vector.tensor_scalar(evidence[:, EV_LO:EV_END], evidence[:, EV_LO:EV_END], 0.0, None,
                                        ALU.mult).then_inc(ev_step, 1)
                dve.wait_ge(ev_step, 1)
                nc.vector.tensor_reduce(ev_sum[:, :], evidence[:, :], AX.X, ALU.add).then_inc(ev_step, 1)

            def verdict(_):
                dve.wait_ge(ev_ps, 1)
                nc.vector.tensor_scalar(clean[:, :], bank[0][0:1, 0:1], 0.0, None, ALU.is_equal).then_inc(clean_ok, 1)

            order = [(SUM_AT, 2, sum_up, 0), (BACK_AT[-1] + 20, 1, verdict, 0)]
            for q in range(LAST):
                order.append((BACK_AT[q], 6, residual, q))
                order.append((BACK_AT[q] + G_LAG, 2, gain, q))
                order.append((BACK_AT[q] + H_LAG, 2, bias, q))
                order.append((BACK_AT[q] + H_LAG + 3, 3, low, q))
            for d in range(NC):
                order.append((BACK_AT[NC + d // 2] + 7, 1, verify_diagonal, d))
            for q in range(LAST, len(ITEMS)):
                order.append((BACK_AT[q], 6, residual, q))
                order.append((BACK_AT[q] + 9, 6, result, q))
            v, now = 0, 0
            for at, length, step, arg in sorted(order, key=lambda entry: entry[0]):
                while v < len(LOWER) and (now + VERIFY <= at or step is sum_up):
                    verify(v)
                    v, now = v + 1, now + VERIFY
                step(arg)
                now = max(now, at) + length
            with unless_clean(dve):
                dve.wait_ge(out_done, 16 * (len(ITEMS) - LAST))
                general_vector(nc, dve, m)

        @block.tensor
        def _(pe):
            def fill_spare(use, k):
                kind, i, n, _ = USES[use]
                if use >= SPARE:
                    engine = USES[use - SPARE][3]
                    pe.wait_ge(read_by[engine], reads(engine, use - SPARE))
                dst = bank[NA + use % SPARE]
                if kind == "xT":
                    pe.wait_ge(relu0_ok, i + 1)
                    for t in range(TC):
                        last = nc.tensor.transpose(dst[:, t * P:(t + 1) * P], x_sb[:, i * TC + t, :], ident[:, :])
                elif kind == "h1":
                    xT_use = USES.index(("xT", i, 0, "act"))
                    pe.wait_ge(read_by["act"], reads("act", xT_use))
                    for t in range(TC):
                        last = nc.tensor.matmul(dst[:, t * E:(t + 1) * E], xT[:, i % 2, t * P:(t + 1) * P],
                                                w_sb[:, 0, :], start=True, stop=True)
                else:
                    k, i = i
                    pe.wait_ge(converted, UPPER_OF[i + n - 1][-1] + 1)
                    for t in range(n):
                        last = nc.tensor.matmul(dst[:, t * P:(t + 1) * P], adj8[:, i + t, k * P:(k + 1) * P],
                                                ident8[:, :], start=True, stop=True)
                last.then_inc(spare_filled, 1)

            def product(q, k, part):
                l, bk, t0, nt = ITEMS[q]
                last = nc.tensor.matmul(bank[bk][:, 0:nt * P], hs_of[l][:, k, part, :],
                                        adj8[:, k, t0 * P:(t0 + nt) * P],
                                        start=(k == 0 and part == 0), stop=(k == T - 1 and part == 1))
                if k == T - 1 and part == 1:
                    last.then_inc(acc_done, 1)

            def accumulate(qs, k):
                for part in range(2):
                    for q in qs:
                        product(q, k, part)

            def diagonal(d):
                if d == 0:
                    pe.wait_ge(lo_ok, NC)
                if d >= 2:
                    pe.wait_ge(diag_ok, d - 1)
                for t in range(TC):
                    k = d * TC + t
                    last = nc.tensor.matmul(bank[NC - 2 + d % 2][:, t * P:(t + 1) * P], adj8[:, k, k * P:(k + 1) * P],
                                            ident8[:, :], start=True, stop=True)
                last.then_inc(diag_ps, 1)

            def back(q):
                _, bk, _, nt = ITEMS[q]
                pe.wait_ge(relu_ok, q + 1)
                for t in range(nt):
                    last = nc.tensor.transpose(bank[bk][:, t * P:(t + 1) * P], reluT[:, q % 2, t * P:(t + 1) * P],
                                               ident[:, :])
                last.then_inc(back_ps, 1)

            def transpose_n(q):
                _, bk, t0, nt = ITEMS[q]
                pe.wait_ge(n_ok, q + 1)
                for t in range(nt):
                    last = nc.tensor.transpose(bank[bk][:, t * P:(t + 1) * P], nres[:, t0 + t, :], ident[:, :])
                last.then_inc(nT_ps, 1)

            def project(q):
                l, bk, _, nt = ITEMS[q]
                pe.wait_ge(nT_ok, q + 1)
                for t in range(nt):
                    last = nc.tensor.matmul(bank[bk][:, t * E:(t + 1) * E], nT[:, 0, t * P:(t + 1) * P],
                                            w_sb[:, l + 1, :], start=True, stop=True)
                last.then_inc(h_ps, 1)

            pe.wait_ge(ident_ok, 1)
            fill_spare(0, 0)
            pe.wait_ge(first_in, 32)
            fill_spare(1, 0)
            pe.wait_ge(const_ok, 1)
            for k in range(T + BEHIND):
                uses = USES_OF[k] if k < T else []
                at_once = AT_ONCE if k >= BEHIND else len(uses)
                for use in uses[:at_once]:
                    fill_spare(use, k)
                uses = uses[at_once:]
                if k < BEHIND:
                    continue
                pe.wait_ge(lo1_ok, k - BEHIND + 1)
                turns = [(n + 1) * 2 * NA // (len(uses) + 1) for n in range(len(uses))]
                n_mm = 0
                for part in range(2):
                    for q in range(NA):
                        for use, turn in zip(uses, turns):
                            if turn == n_mm:
                                fill_spare(use, k)
                        product(q, k - BEHIND, part)
                        n_mm += 1

            due = {}
            for q in range(len(ITEMS) - 1):
                due.setdefault(BACK_AT[q], []).append((back, q))
                if q < LAST:
                    due.setdefault(BACK_AT[q] + N_LAG, []).append((transpose_n, q))
                    due.setdefault(BACK_AT[q] + H_LAG, []).append((project, q))
            for d in range(NC):
                due.setdefault(BACK_AT[NC + d // 2] + 1, []).append((diagonal, d))
            g = 0

            def products(qs, k):
                nonlocal g
                accumulate(qs, k)
                for _ in qs:
                    g += 1
                    for step, q in due.pop(g, ()):
                        step(q)

            for q in range(NA, NC):
                if q == NA:
                    pe.wait_ge(params_in, 16 * (4 * LAYERS - 2))
                    for engine in ("act", "dve"):
                        pe.wait_ge(read_by[engine], reads(engine, len(USES)))
                for k in range(T):
                    products([q], k)
            for e in range(NC):
                pe.wait_ge(lo_ok, e + 1)
                for k in range(e * TC, (e + 1) * TC):
                    if e:
                        products(list(range(NC, NC + min(e, WIDE))), k)
                if e < WIDE:
                    for k in range((e + 1) * TC):
                        products([NC + e], k)
            for q in range(NC + WIDE, LAST):
                if ITEMS[q][1] == NC - 2:
                    pe.wait_ge(diag_ok, NC)
                for k in range(T):
                    products([q], k)
            for k in range(T):
                if k % TC == 0:
                    pe.wait_ge(lo_ok, NC + k // TC + 1)
                products([LAST, LAST + 1], k)
            for q in range(LAST + 2, len(ITEMS)):
                if q == len(ITEMS) - 1:
                    pe.wait_ge(y_ok, q - 2)
                for k in range(T):
                    products([q], k)
            assert not due, due
            back(len(ITEMS) - 1)
            pe.wait_ge(ev_step, 2)
            nc.tensor.matmul(bank[0][0:1, 0:1], ev_sum[:, :], ones[:, :], start=True, stop=True).then_inc(ev_ps, 1)
            with unless_clean(pe):
                general_tensor(nc, pe, m)


_PARAMS = ["W", "b", "g", "be"]


def kernel(**inputs):
    import numpy as _np
    import concourse.bacc as _bacc
    from concourse import mybir as _mybir
    from concourse.bass_utils import run_bass_kernel_spmd as _run

    nc = _bacc.Bacc("TRN2", target_bir_lowering=False, num_devices=1)
    arrays, aps = {}, {}
    for name in ["x", "adj"] + [f"L0_gnn_{p}{l + 1}" for p in _PARAMS for l in range(LAYERS)]:
        a = _np.ascontiguousarray(inputs[name])
        arrays[f"in_{name}"] = a
        aps[name] = nc.dram_tensor(f"in_{name}", a.shape, _mybir.dt.from_np(a.dtype), kind="ExternalInput").ap()
    out = nc.dram_tensor("out_0", (N, E), _mybir.dt.float32, kind="ExternalOutput").ap()
    w, b, g, be = ([aps[f"L0_gnn_{p}{l + 1}"] for l in range(LAYERS)] for p in _PARAMS)
    build(nc, aps["x"], aps["adj"], w, b, g, be, out)
    r = _run(nc, [arrays], core_ids=[0])
    return r.results[0]["out_0"]
```

```python
from contextlib import ExitStack

import concourse.bass as bass
from concourse import mybir

FP32 = mybir.dt.float32
FP16 = mybir.dt.float16
FP8 = mybir.dt.float8e4
I32 = mybir.dt.int32
ALU = mybir.AluOpType
ACT = mybir.ActivationFunctionType
AX = mybir.AxisListType

P = 128
N = 4096
E = 128
T = N // P
CW = 512
NC = N // CW
TC = CW // P
LAYERS = 3
EPS = 1e-5
HS_SCALE = 4096.0

UNIT = 2048
SLOTS = 4
UPPER = [(k, c, min(UNIT, N - c)) for k in range(T) for c in range(k * P, N, UNIT)]
UPPER_OF = [[u for u, (kk, _, _) in enumerate(UPPER) if kk == k] for k in range(T)]
LUNIT = 512
LSLOTS = 5
LOWER = [(k, c, min(LUNIT, k * P - c)) for k in range(T) for c in range(0, k * P, LUNIT)]
PARTS = 16
NA = 5
XPARTS = 4
XT = T // XPARTS
X_BEFORE = [5, 8, 16]
PARAMS_BEFORE = [20, 26, 34]

SPARE = NC - NA
AHEAD = 4
BEHIND = 2
AT_ONCE = 2
SCALED = 1
ACT_COL, ACT_ROW, DVE_COL, DVE_ROW = 1.6e-3, 0.5, 1.8e-3, 1.8
WORK = {"act": 0.0, "dve": 0.0}
USES, USES_OF, LAST_MIRROR = [("xT", 0, 0, TC, "act"), ("h1", 0, 0, TC, "dve")], [], [None] * T
_left = [(k, j) for k in range(T) for j in range(0, k, TC)]
for _k in range(T):
    _first = len(USES)
    WORK["act"] += ACT_COL * (N - _k * P) + ACT_ROW
    WORK["dve"] += DVE_COL * (N - _k * P) + DVE_ROW
    if _k // TC + 1 < NC:
        if _k % TC == 1:
            USES.append(("xT", _k // TC + 1, 0, TC, "act"))
        if _k % TC == 2:
            USES.append(("h1", _k // TC + 1, 0, TC, "dve"))
    for _to, _j in list(_left):
        if _to == _k or (len(USES) - _first < AHEAD and _to < T - 5 and _j + TC <= min(_k, _to)):
            _left.remove((_to, _j))
            LAST_MIRROR[_to] = len(USES)
            _engine = min(WORK, key=WORK.get)
            WORK[_engine] += 1
            USES.append(("mirror", _to, _j, min(TC, _to - _j), _engine))
    USES_OF.append(list(range(_first, len(USES))))


def reads(engine, use):
    return sum(u[-1] == engine for u in USES[:use + 1])


ITEMS = [(l, c, c * TC, TC) for l in range(LAYERS) for c in range(NC)]
_l, _c, _t, _n = ITEMS.pop()
ITEMS += [(_l, _c, _t, _n // 2), (_l, _c - 2, _t + _n // 2, _n // 2)]
LAST = 2 * NC
PACE, G_LAG, N_LAG, H_LAG, VERIFY = 12, 14, 27, 31, 2
WIDE = 4

FIRST_AT = [0] * NA + [(q - NA + 1) * T for q in range(NA, NC)]
FIRST_AT += [(NC - NA + max(WIDE, q - NC + 1)) * T for q in range(NC, LAST)]
FIRST_AT += [FIRST_AT[-1] + max(2, q - LAST + 1) * T for q in range(LAST, len(ITEMS))]
BACK_AT = []
for _q, _f in enumerate(FIRST_AT):
    _at = max(_f + 3, BACK_AT[-1] + (PACE if _q < LAST else 4) if BACK_AT else 0)
    BACK_AT.append(_at)
SUM_AT = BACK_AT[-2] + 18

TENSOR_DUE = {}
for _q in range(len(ITEMS) - 1):
    TENSOR_DUE.setdefault(BACK_AT[_q], []).append(("back", _q))
    if _q < LAST:
        TENSOR_DUE.setdefault(BACK_AT[_q] + N_LAG, []).append(("transpose_n", _q))
        TENSOR_DUE.setdefault(BACK_AT[_q] + H_LAG, []).append(("project", _q))
for _d in range(NC):
    TENSOR_DUE.setdefault(BACK_AT[NC + _d // 2] + 1, []).append(("diagonal", _d))
SCALAR_STEPS = []
for _q in range(LAST):
    SCALAR_STEPS += [(max(FIRST_AT[_q], BACK_AT[_q] - 10), "relu_out", _q), (BACK_AT[_q] + 12, "standardise", _q),
                     (BACK_AT[_q] + N_LAG, "copy_nT", _q), (BACK_AT[_q] + H_LAG + 2, "high", _q)]
SCALAR_STEPS.sort(key=lambda s: s[0])
SCALAR_STEPS += [(BACK_AT[_q], "relu_out", _q) for _q in range(LAST, len(ITEMS))]
_steps = [(SUM_AT, 2, "sum_up", 0), (BACK_AT[-1] + 20, 1, "verdict", 0)]
for _q, _at in enumerate(BACK_AT):
    _steps.append((_at, 6, "residual", _q))
    if _q < LAST:
        _steps += [(_at + G_LAG, 2, "gain", _q), (_at + H_LAG, 2, "bias", _q), (_at + H_LAG + 3, 3, "low", _q)]
    else:
        _steps.append((_at + 9, 6, "result", _q))
for _d in range(NC):
    _steps.append((BACK_AT[NC + _d // 2] + 7, 1, "verify_diagonal", _d))
VECTOR_STEPS, _v, _now = [], 0, 0
for _at, _length, _step, _q in sorted(_steps, key=lambda s: s[0]):
    while _v < len(LOWER) and (_now + VERIFY <= _at or _step == "sum_up"):
        VECTOR_STEPS.append(("verify", _v))
        _v, _now = _v + 1, _now + VERIFY
    VECTOR_STEPS.append((_step, _q))
    _now = max(_now, _at) + _length

EV_UPPER = 0
EV_LOWER = EV_UPPER + len(UPPER)
EV_DIAG = EV_LOWER + len(LOWER)
EV_LO = EV_DIAG + NC
EV_END = EV_LO + LAYERS * T


_NORM = ["y", "stats", "moments", "variance", "rstd", "centred"]
_NEXT = ["n_transposed", "nT_copied", "projected", "h", "h_kept", "h_scaled", "hs_stored"]
_LAYER = ["row_transposed", "rowT_copied", "summed", "dinv_fetched", "residual_fetched", "scaled"]
STEPS = ([["row_summed", "dinv_found", "dinv_kept"] + _NORM + ["n"] + _NEXT]
         + [_LAYER + _NORM + ["gained", "n"] + _NEXT] * (LAYERS - 1)
         + [_LAYER + _NORM + ["gained", "n", "result"]])


def tile_begins(stage, i):
    return i * len(STEPS[stage]) + (1 + T * sum(len(STEPS[s]) for s in range(stage)))


def after(stage, i, step):
    return tile_begins(stage, i) + (STEPS[stage].index(step) + 1)


def general_sync(nc, sp, m):
    for stage in range(LAYERS + 1):
        with sp.Fori(0, T) as i:
            sp.wait_ge(m.step, tile_begins(stage, i))
            sp.dma_start(m.row[:, :], m.adj[bass.ts(i, P), :]).then_inc(m.row_in, 16)
            if stage in (0, LAYERS):
                sp.dma_start(m.xt[:, :], m.x[bass.ts(i, P), :]).then_inc(m.x_in, 16)
            if stage == LAYERS:
                sp.wait_ge(m.step, after(stage, i, "result"))
                sp.dma_start(m.out[bass.ts(i, P), :], m.result[:, :]).then_inc(m.stored, 16)
    sp.wait_ge(m.stored, 16 * T)


def general_tensor(nc, pe, m):
    for stage in range(LAYERS + 1):
        with pe.Fori(0, T) as i:
            if stage:
                pe.wait_ge(m.row_in, (i + (stage * T + 1)) * 16)
                for k in range(T):
                    last = nc.tensor.transpose(m.bank[k // TC][:, (k % TC) * P:(k % TC + 1) * P],
                                               m.row[:, k * P:(k + 1) * P], m.ident[:, :])
                last.then_inc(m.step, 1)
                pe.wait_ge(m.step, after(stage, i, "rowT_copied"))
                for k in range(T):
                    last = nc.tensor.matmul(m.bank[0][:, 0:E], m.rowT[:, k, :], m.hs[(stage - 1) % 2][:, k, :],
                                            start=(k == 0), stop=(k == T - 1))
                last.then_inc(m.step, 1)
            if stage < LAYERS:
                pe.wait_ge(m.step, after(stage, i, "n"))
                nc.tensor.transpose(m.bank[1][:, 0:P], m.n[:, :], m.ident[:, :]).then_inc(m.step, 1)
                pe.wait_ge(m.step, after(stage, i, "nT_copied"))
                nc.tensor.matmul(m.bank[2][:, 0:E], m.nT[:, :], m.w[:, stage, :], start=True,
                                 stop=True).then_inc(m.step, 1)


def general_scalar(nc, act, m):
    for stage in range(LAYERS + 1):
        with act.Fori(0, T) as i:
            if stage:
                act.wait_ge(m.step, after(stage, i, "row_transposed"))
                for c in range(NC):
                    last = nc.scalar.activation(m.rowT[:, c * TC:(c + 1) * TC, :], m.tiles(m.bank[c][:, :]), ACT.Copy)
                last.then_inc(m.step, 1)
            if stage < LAYERS:
                act.wait_ge(m.step, after(stage, i, "n_transposed"))
                nc.scalar.activation(m.nT[:, :], m.bank[1][:, 0:P], ACT.Copy).then_inc(m.step, 1)


def general_pool(nc, pool, m):
    for stage in range(LAYERS + 1):
        with pool.Fori(0, T) as i:
            if stage == 0:
                pool.wait_ge(m.step, after(stage, i, "row_summed"))
                nc.gpsimd.tensor_tensor(m.dinv_i[:, :], m.rowsum_i[:, :], m.mhalf[:, 0:1], ALU.pow).then_inc(m.step, 1)
            pool.wait_ge(m.step, after(stage, i, "moments"))
            nc.gpsimd.tensor_tensor(m.var[:, :], m.mv[:, 1:2], m.eps[:, :], ALU.add).then_inc(m.step, 1)
            pool.wait_ge(m.step, after(stage, i, "variance"))
            nc.gpsimd.tensor_tensor(m.rstd[:, :], m.var[:, :], m.mhalf[:, 0:1], ALU.pow).then_inc(m.step, 1)


def general_vector(nc, dve, m):
    def carry():
        nc.vector.memset(m.carrier[:, :], 0.0)

    nc.vector.memset(m.eps[:, :], EPS).then_inc(m.step, 1)
    for stage in range(LAYERS + 1):
        with dve.Fori(0, T) as i:
            def then(ins, step):
                ins.then_inc(m.step, 1)
                dve.wait_ge(m.step, after(stage, i, step))

            if stage:
                dve.wait_ge(m.step, after(stage, i, "summed"))
                carry()
                then(nc.vector.tensor_copy(m.dinv_i[:, :], m.dinv[:, bass.ds(i, 1)]), "dinv_fetched")
                carry()
                then(nc.vector.tensor_copy(m.res_i[:, :], m.res[:, bass.ds(i, 1), :]), "residual_fetched")
                then(nc.vector.tensor_scalar(m.y[:, :], m.bank[0][:, 0:E], m.dinv_i[:, :], 0.0, ALU.mult, ALU.max),
                     "scaled")
                then(nc.vector.tensor_tensor(m.y[:, :], m.y[:, :], m.res_i[:, :], ALU.add), "y")
            else:
                dve.wait_ge(m.x_in, (i + 1) * 16)
                dve.wait_ge(m.row_in, (i + 1) * 16)
                dve.wait_ge(m.step, tile_begins(stage, i))
                then(nc.vector.tensor_reduce(m.rowsum_i[:, :], m.row[:, :], AX.X, ALU.add), "row_summed")
                dve.wait_ge(m.step, after(stage, i, "dinv_found"))
                carry()
                then(nc.vector.tensor_copy(m.dinv[:, bass.ds(i, 1)], m.dinv_i[:, :]), "dinv_kept")
                then(nc.vector.tensor_copy(m.y[:, :], m.xt[:, :]), "y")
            then(nc.vector.bn_stats(m.st[:, :], m.y[:, :]), "stats")
            carry()
            then(nc.vector.bn_aggr(m.mv[:, :], m.st[:, :]), "moments")
            dve.wait_ge(m.step, after(stage, i, "rstd"))
            then(nc.vector.tensor_scalar(m.y[:, :], m.y[:, :], m.mv[:, 0:1], m.rstd[:, :], ALU.subtract, ALU.mult),
                 "centred")
            if stage:
                then(nc.vector.tensor_tensor(m.y[:, :], m.y[:, :], m.g[:, stage - 1, :], ALU.mult), "gained")
                then(nc.vector.tensor_tensor(m.n[:, :], m.y[:, :], m.be[:, stage - 1, :], ALU.add), "n")
            else:
                then(nc.vector.tensor_scalar(m.n[:, :], m.y[:, :], 0.0, None, ALU.max), "n")
            if stage < LAYERS:
                dve.wait_ge(m.step, after(stage, i, "projected"))
                then(nc.vector.tensor_tensor(m.h[:, :], m.bank[2][:, 0:E], m.b[:, stage, :], ALU.add), "h")
                kept = m.n if stage else m.h
                carry()
                then(nc.vector.tensor_copy(m.res[:, bass.ds(i, 1), :], kept[:, :]), "h_kept")
                then(nc.vector.tensor_scalar(m.h[:, :], m.h[:, :], m.dinv_i[:, :], None, ALU.mult), "h_scaled")
                carry()
                then(nc.vector.tensor_copy(m.hs[stage % 2][:, bass.ds(i, 1), :], m.h[:, :]), "hs_stored")
            else:
                dve.wait_ge(m.x_in, (i + T + 1) * 16)
                then(nc.vector.tensor_tensor(m.result[:, :], m.n[:, :], m.xt[:, :], ALU.add), "result")


def build(nc, x, adj, w, b, g, be, out):
    x_v = x.rearrange("(t p) e -> p t e", p=P)
    out_v = out.rearrange("(t p) e -> p t e", p=P)
    adj_v = adj.rearrange("(t p) n -> t p n", p=P)

    ctx = ExitStack()
    with ctx:
        def sb(name, shape, dt):
            return ctx.enter_context(nc.sbuf_tensor(name, shape, dt))

        def sem(name):
            return ctx.enter_context(nc.semaphore(name))

        adj8 = sb("adj8", [P, T, N], FP8)
        room = sb("room", [P, SLOTS * UNIT + UNIT // 2], FP32)
        nres = sb("nres", [P, T, E], FP32)
        hs_a = sb("hs_a", [P, T, 2, E], FP16)
        ident = sb("ident", [P, P], FP32)
        ident8 = sb("ident8", [P, P], FP8)
        w_sb = sb("w_sb", [P, LAYERS, E], FP32)
        b_bc = sb("b_bc", [P, LAYERS, E], FP32)
        g_bc = sb("g_bc", [P, LAYERS, E], FP32)
        be_bc = sb("be_bc", [P, LAYERS, E], FP32)
        evidence = sb("evidence", [P, EV_END], FP32)
        rs_part = sb("rs_part", [P, T, PARTS], FP32)
        rowsum = sb("rowsum", [P, T], FP32)
        dinv = sb("dinv", [P, T], FP32)
        dinv_in = sb("dinv_in", [P, T], FP32)
        dinv_out = sb("dinv_out", [P, T], FP32)
        mhalf = sb("mhalf", [P, TC], FP32)
        ones = sb("ones", [P, 1], FP32)
        st0 = sb("st0", [P, TC, 6], FP32)
        mv0 = sb("mv0", [P, TC, 2], FP32)
        var0 = sb("var0", [P, TC], FP32)
        rstd0 = sb("rstd0", [P, T], FP32)
        st = sb("st", [P, TC, 6], FP32)
        mv = sb("mv", [P, 2, TC, 2], FP32)
        vare = sb("vare", [P, 2, TC], FP32)
        rstd = sb("rstd", [P, 2, TC], FP32)
        nmean = sb("nmean", [P, 2, TC], FP32)
        nmr = sb("nmr", [P, 2, TC], FP32)
        ev_sum = sb("ev_sum", [P, 1], FP32)
        tick = sb("tick", [P, 1], FP32)
        clean = sb("clean", [1, 1], I32)

        x_sb = adj8[:, T - 4:T, :].rearrange("p a n -> p (a n)").bitcast(FP32).rearrange("p (t e) -> p t e", e=E)
        xT = adj8[:, T - 5:T - 4, :].rearrange("p a n -> p (a n)").bitcast(FP32).rearrange("p (s n) -> p s n", n=CW)
        stage = room[:, 0:SLOTS * UNIT].rearrange("p (s n) -> p s n", n=UNIT)
        junk = room[:, SLOTS * UNIT:].bitcast(FP8).rearrange("p (s n) -> p s n", n=UNIT)
        hs_b = room[:, 0:N].bitcast(FP16).rearrange("p (t h e) -> p t h e", h=2, e=E)
        xb = room[:, 0:N].rearrange("p (t e) -> p t e", e=E)

        def tiles_of(t):
            return t[:, :].rearrange("p (t e) -> p t e", e=E)

        def slots(first, n, width):
            return room[:, first:first + n * width].rearrange("p (s n) -> p s n", n=width)

        reluT = slots(N, 2, CW)
        yb = slots(N + 2 * CW, 2, CW)
        nT = slots(N + 4 * CW, 1, CW)
        hb = slots(N + 5 * CW, 1, CW)
        lstage = slots(N + 6 * CW, LSLOTS - 1, LUNIT)
        lslot = [lstage[:, i, :] for i in range(LSLOTS - 1)] + [rs_part[:, :, :].rearrange("p t n -> p (t n)")]
        diag_out = tiles_of(sb("diag_out", [P, CW], FP8))
        hs_of = [hs_a, hs_b, hs_a]

        bank = [ctx.enter_context(nc.psum_tensor(f"bank{i}", [P, CW], FP32)) for i in range(NC)]

        def tiles(ap):
            return ap.rearrange("p (t e) -> p t e", e=E)

        x_in = [sem(f"x_in{i}") for i in range(XPARTS)]
        first_in = sem("first_in")
        params_in = sem("params_in")
        x_again = sem("x_again")
        slot_in = [sem(f"slot_in{i}") for i in range(SLOTS)]
        ident_0 = sem("ident_0")
        ident_ok = sem("ident_ok")
        const_ok = sem("const_ok")
        converted = sem("converted")
        checked = sem("checked")
        lslot_in = [sem(f"lslot_in{i}") for i in range(LSLOTS)]
        verified = sem("verified")
        spare_filled = sem("spare_filled")
        read_by = {"act": sem("spare_read_act"), "dve": sem("spare_read_dve")}
        parts_zero = sem("parts_zero")
        diag_ps = sem("diag_ps")
        diag_ok = sem("diag_ok")
        pool_step = sem("pool_step")
        dinv_ok = sem("dinv_ok")
        dout_ok = sem("dout_ok")
        stat0 = sem("stat0")
        mv0_ok = sem("mv0_ok")
        rstd0_ok = sem("rstd0_ok")
        relu0_ok = sem("relu0_ok")
        h1_ok = sem("h1_ok")
        hi1_ok = sem("hi1_ok")
        lo1_ok = sem("lo1_ok")
        acc_done = sem("acc_done")
        relu_ok = sem("relu_ok")
        back_ps = sem("back_ps")
        y_ok = sem("y_ok")
        stat_ok = sem("stat_ok")
        mv_ok = sem("mv_ok")
        rstd_ok = sem("rstd_ok")
        nmean_ok = sem("nmean_ok")
        z_ok = sem("z_ok")
        zg_ok = sem("zg_ok")
        n_ok = sem("n_ok")
        nT_ps = sem("nT_ps")
        nT_ok = sem("nT_ok")
        h_ps = sem("h_ps")
        h_ok = sem("h_ok")
        hi_ok = sem("hi_ok")
        lo_ok = sem("lo_ok")
        xb_ok = sem("xb_ok")
        ev_step = sem("ev_step")
        ev_ps = sem("ev_ps")
        clean_ok = sem("clean_ok")
        out_done = sem("out_done")

        class General:
            pass

        m = General()
        taken = [0]

        def place(cols):
            first = taken[0]
            taken[0] += cols
            return adj8[:, :, :].rearrange("p t n -> p (t n)").bitcast(FP32)[:, first:taken[0]]

        m.x, m.adj, m.out = x, adj, out
        m.row = place(N)
        m.rowT = place(N).rearrange("p (t n) -> p t n", n=P)
        m.hs = [place(N).rearrange("p (t n) -> p t n", n=E) for _ in range(2)]
        m.xt, m.y, m.res_i, m.n, m.nT, m.h, m.result = (place(E) for _ in range(7))
        m.dinv_i, m.rowsum_i, m.var, m.rstd, m.eps, m.carrier = (place(1) for _ in range(6))
        m.st, m.mv = place(6), place(2)
        m.res, m.dinv, m.ident, m.mhalf = nres, dinv, ident, mhalf
        m.w, m.b, m.g, m.be, m.bank, m.tiles = w_sb, b_bc, g_bc, be_bc, bank, tiles
        m.step = sem("general_step")
        m.row_in = sem("general_row_in")
        m.x_in = sem("general_x_in")
        m.stored = sem("general_stored")

        def unless_clean(eng):
            eng.wait_ge(clean_ok, 1)
            verdict = eng.alloc_register()
            eng.reg_load(verdict, clean[0:1, 0:1])
            return eng.If_eq(verdict, 0)

        block = ctx.enter_context(nc.Block())

        @block.sync
        def _(sp):
            for u, (k, c0, width) in enumerate(UPPER):
                if u in X_BEFORE:
                    i = X_BEFORE.index(u) + 1
                    sp.dma_start(x_sb[:, i * XT:(i + 1) * XT, :],
                                 x_v[:, i * XT:(i + 1) * XT, :]).then_inc(x_in[i], 16)
                if u in PARAMS_BEFORE:
                    l = PARAMS_BEFORE.index(u)
                    if l:
                        sp.dma_start(w_sb[:, l, :], w[l]).then_inc(params_in, 16)
                        sp.dma_start(b_bc[:, l, :], b[l].partition_broadcast(P)).then_inc(params_in, 16)
                    sp.dma_start(g_bc[:, l, :], g[l].partition_broadcast(P)).then_inc(params_in, 16)
                    sp.dma_start(be_bc[:, l, :], be[l].partition_broadcast(P)).then_inc(params_in, 16)
                if u >= SLOTS:
                    sp.wait_ge(converted, u - SLOTS + 1)
                    sp.wait_ge(checked, u - SLOTS + 1)
                sp.dma_start(stage[:, u % SLOTS, 0:width],
                             adj_v[k, :, c0:c0 + width]).then_inc(slot_in[u % SLOTS], 16)
            for v, (k, c0, width) in enumerate(LOWER):
                if v == LSLOTS - 1:
                    sp.wait_ge(dout_ok, 1)
                if v == 0:
                    sp.wait_ge(converted, len(UPPER))
                    sp.wait_ge(checked, len(UPPER))
                if v >= LSLOTS:
                    sp.wait_ge(verified, v - LSLOTS + 1)
                sp.dma_start(lslot[v % LSLOTS][:, 0:width],
                             adj_v[k, :, c0:c0 + width]).then_inc(lslot_in[v % LSLOTS], 16)
            for q in range(LAST, len(ITEMS)):
                _, _, t0, nt = ITEMS[q]
                sp.wait_ge(n_ok, q + 1)
                sp.dma_start(out_v[:, t0:t0 + nt, :], nres[:, t0:t0 + nt, :]).then_inc(out_done, 16)
            sp.wait_ge(out_done, 16 * (len(ITEMS) - LAST))
            with unless_clean(sp):
                general_sync(nc, sp, m)

        @block.gpsimd
        def _(pool):
            steps = [0]

            def chain(ins):
                steps[0] += 1
                ins.then_inc(pool_step, 1)
                pool.wait_ge(pool_step, steps[0])

            nc.gpsimd.memset(ident[:, :], 0.0).then_inc(ident_0, 1)
            nc.gpsimd.memset(mhalf[:, :], -0.5)
            nc.gpsimd.memset(rs_part[:, :, :], 0.0).then_inc(parts_zero, 1)
            nc.gpsimd.memset(ones[:, :], 1.0)
            pool.wait_ge(ident_0, 1)
            nc.gpsimd.affine_select(out=ident[:, :], in_=ident[:, :], compare_op=ALU.not_equal, fill=1.0,
                                    base=0, pattern=[[-1, P]], channel_multiplier=1).then_inc(ident_ok, 1)
            pool.wait_ge(ident_ok, 1)

            def rstd_of_x(i):
                pool.wait_ge(mv0_ok, i + 1)
                chain(nc.gpsimd.tensor_scalar(var0[:, :], mv0[:, :, 1], EPS, None, ALU.add))
                nc.gpsimd.tensor_tensor(rstd0[:, i * TC:(i + 1) * TC], var0[:, :], mhalf[:, :],
                                        ALU.pow).then_inc(rstd0_ok, 1)

            rstd_of_x(0)
            for k in range(T):
                if k % TC == 0 and k // TC + 1 < NC:
                    rstd_of_x(k // TC + 1)
                pool.wait_ge(converted, UPPER_OF[k][-1] + 1)
                if k:
                    for engine in ("act", "dve"):
                        if reads(engine, LAST_MIRROR[k]):
                            pool.wait_ge(read_by[engine], reads(engine, LAST_MIRROR[k]))
                width = PARTS // 2
                while width > 1:
                    chain(nc.gpsimd.tensor_tensor(rs_part[:, k, 0:width], rs_part[:, k, 0:width],
                                                  rs_part[:, k, width:2 * width], ALU.add))
                    width //= 2
                chain(nc.gpsimd.tensor_tensor(rowsum[:, k:k + 1], rs_part[:, k, 0:1], rs_part[:, k, 1:2], ALU.add))
                chain(nc.gpsimd.tensor_tensor(dinv[:, k:k + 1], rowsum[:, k:k + 1], mhalf[:, 0:1], ALU.pow))
                nc.gpsimd.tensor_scalar(dinv_in[:, k:k + 1], dinv[:, k:k + 1], HS_SCALE, None,
                                        ALU.mult).then_inc(dinv_ok, 1)
            nc.gpsimd.tensor_scalar(dinv_out[:, :], dinv[:, :], 1.0 / HS_SCALE, None, ALU.mult).then_inc(dout_ok, 1)

            def shift(q):
                l, _, t0, nt = ITEMS[q]
                pool.wait_ge(zg_ok, q + 1)
                nc.gpsimd.tensor_tensor(nres[:, t0:t0 + nt, :], tiles(yb[:, q % 2, :])[:, 0:nt, :],
                                        be_bc[:, l:l + 1, :].to_broadcast([P, nt, E]), ALU.add).then_inc(n_ok, 1)

            for q in range(len(ITEMS)):
                l, _, _, nt = ITEMS[q]
                if q == LAST:
                    pool.wait_ge(acc_done, LAST)
                    pool.dma_start(xb, x_v).then_inc(x_again, 16)
                    pool.wait_ge(x_again, 16)
                    nc.gpsimd.tensor_tensor(xb, xb, be_bc[:, LAYERS - 1:LAYERS, :].to_broadcast([P, T, E]),
                                            ALU.add).then_inc(xb_ok, 1)
                pool.wait_ge(mv_ok, q + 1)
                if q >= 2:
                    pool.wait_ge(z_ok, q - 1)
                chain(nc.gpsimd.tensor_scalar(vare[:, q % 2, 0:nt], mv[:, q % 2, 0:nt, 1], EPS, None, ALU.add))
                last = nc.gpsimd.tensor_tensor(rstd[:, q % 2, 0:nt], vare[:, q % 2, 0:nt], mhalf[:, 0:nt], ALU.pow)
                if q < LAST:
                    chain(last)
                    pool.wait_ge(nmean_ok, q + 1)
                    last = nc.gpsimd.tensor_tensor(nmr[:, q % 2, :], nmean[:, q % 2, :], rstd[:, q % 2, :], ALU.mult)
                last.then_inc(rstd_ok, 1)
                if q < LAST:
                    shift(q)
            with unless_clean(pool):
                general_pool(nc, pool, m)

        @block.scalar
        def _(act):
            act.dma_start(x_sb[:, 0:XT, :], x_v[:, 0:XT, :]).then_inc(x_in[0], 16)
            act.dma_start(w_sb[:, 0, :], w[0]).then_inc(first_in, 16)
            act.dma_start(b_bc[:, 0, :], b[0].partition_broadcast(P)).then_inc(first_in, 16)

            def convert(u):
                k, c0, width = UPPER[u]
                act.wait_ge(slot_in[u % SLOTS], 16 * (u // SLOTS + 1))
                nc.scalar.activation(adj8[:, k, c0:c0 + width], stage[:, u % SLOTS, 0:width], ACT.Copy,
                                     accum_out=rs_part[:, k, u - UPPER_OF[k][0]:u - UPPER_OF[k][0] + 1],
                                     saturate=False).then_inc(converted, 1)

            def read_spare(use):
                kind, i, j, n, engine = USES[use]
                if engine != "act":
                    return
                act.wait_ge(spare_filled, use + 1)
                src = bank[NA + use % SPARE]
                if kind == "xT":
                    if i >= 2:
                        act.wait_ge(h1_ok, i - 1)
                    nc.scalar.activation(xT[:, i % 2, :], src[:, :], ACT.Copy).then_inc(read_by["act"], 1)
                else:
                    nc.scalar.activation(adj8[:, i, j * P:(j + n) * P], src[:, 0:n * P], ACT.Copy,
                                         accum_out=rs_part[:, i, 2 + j // TC:3 + j // TC],
                                         saturate=False).then_inc(read_by["act"], 1)

            def high_1(k):
                act.wait_ge(dinv_ok, k + 1)
                act.wait_ge(h1_ok, k // TC + 1)
                nc.scalar.activation(hs_a[:, k, 0, :], nres[:, k, :], ACT.Copy,
                                     scale=dinv_in[:, k:k + 1]).then_inc(hi1_ok, 1)

            act.wait_ge(parts_zero, 1)
            for k in range(T):
                if k == T - 5:
                    act.wait_ge(h1_ok, NC)
                uses, units = USES_OF[k], UPPER_OF[k]
                half = (len(uses) + 1) // 2
                convert(units[0])
                for use in uses[:half]:
                    read_spare(use)
                if k >= SCALED:
                    high_1(k - SCALED)
                for u in units[1:]:
                    convert(u)
                if k == 0:
                    read_spare(0)
                for use in uses[half:]:
                    read_spare(use)
            for k in range(T - SCALED, T):
                high_1(k)

            def relu_out(q):
                _, bk, _, nt = ITEMS[q]
                act.wait_ge(acc_done, q + 1)
                if q == 0:
                    act.wait_ge(checked, len(UPPER))
                if q >= 2:
                    act.wait_ge(back_ps, q - 1)
                nc.scalar.activation(reluT[:, q % 2, 0:nt * P], bank[bk][:, 0:nt * P], ACT.Relu).then_inc(relu_ok, 1)

            def standardise(q):
                act.wait_ge(rstd_ok, q + 1)
                y = tiles(yb[:, q % 2, :])
                for t in range(TC):
                    last = nc.scalar.activation(y[:, t, :], y[:, t, :], ACT.Identity, bias=nmr[:, q % 2, t:t + 1],
                                                scale=rstd[:, q % 2, t:t + 1])
                last.then_inc(z_ok, 1)

            def copy_nT(q):
                act.wait_ge(nT_ps, q + 1)
                if q:
                    act.wait_ge(h_ps, q)
                nc.scalar.activation(nT[:, 0, :], bank[ITEMS[q][1]][:, :], ACT.Copy).then_inc(nT_ok, 1)

            def high(q):
                l, _, t0, nt = ITEMS[q]
                act.wait_ge(h_ok, q + 1)
                for t in range(nt):
                    k = t0 + t
                    last = nc.scalar.activation(hs_of[l + 1][:, k, 0, :], tiles(hb[:, 0, :])[:, t, :], ACT.Copy,
                                                scale=dinv_in[:, k:k + 1])
                last.then_inc(hi_ok, 1)

            for _, step, q in SCALAR_STEPS:
                if step == "relu_out":
                    relu_out(q)
                elif step == "standardise":
                    standardise(q)
                elif step == "copy_nT":
                    copy_nT(q)
                elif step == "high":
                    high(q)
            with unless_clean(act):
                general_scalar(nc, act, m)

        @block.vector
        def _(dve):
            def check(u):
                _, _, width = UPPER[u]
                dve.wait_ge(slot_in[u % SLOTS], 16 * (u // SLOTS + 1))
                if u >= 2:
                    dve.wait_ge(checked, u - 1)
                src = stage[:, u % SLOTS, 0:width]
                nc.vector.scalar_tensor_tensor(out=junk[:, u % 2, 0:width], in0=src, scalar=1.0, in1=src,
                                               op0=ALU.is_equal, op1=ALU.not_equal,
                                               accum_out=evidence[:, EV_UPPER + u:EV_UPPER + u + 1],
                                               saturate=False).then_inc(checked, 1)

            def verify(v):
                k, c0, width = LOWER[v]
                dve.wait_ge(lslot_in[v % LSLOTS], 16 * (v // LSLOTS + 1))
                src = lslot[v % LSLOTS][:, 0:width]
                nc.vector.scalar_tensor_tensor(out=src, in0=src, scalar=1.0, in1=adj8[:, k, c0:c0 + width],
                                               op0=ALU.mult, op1=ALU.not_equal,
                                               accum_out=evidence[:, EV_LOWER + v:EV_LOWER + v + 1]
                                               ).then_inc(verified, 1)

            def verify_diagonal(d):
                dve.wait_ge(diag_ps, d + 1)
                if d:
                    dve.wait_ge(diag_ok, d)
                first = d * TC * (T + 1)
                own = adj8[:, :, :].rearrange("p t (s n) -> p (t s) n", n=P)[:, first:first + (TC - 1) * (T + 1) + 1:T + 1, :]
                nc.vector.scalar_tensor_tensor(out=diag_out, in0=tiles(bank[NC - 2 + d % 2][:, :]), scalar=1.0, in1=own,
                                               op0=ALU.mult, op1=ALU.not_equal,
                                               accum_out=evidence[:, EV_DIAG + d:EV_DIAG + d + 1],
                                               saturate=False).then_inc(diag_ok, 1)

            def norm_x(i):
                if i % (NC // XPARTS) == 0:
                    dve.wait_ge(x_in[i // (NC // XPARTS)], 16)
                for t in range(TC):
                    last = nc.vector.bn_stats(st0[:, t, :], x_sb[:, i * TC + t, :])
                last.then_inc(stat0, 1)
                dve.wait_ge(stat0, i + 1)
                if i:
                    dve.wait_ge(rstd0_ok, i)
                for t in range(TC):
                    last = nc.vector.bn_aggr(mv0[:, t, :], st0[:, t, :])
                last.then_inc(mv0_ok, 1)
                dve.wait_ge(mv0_ok, i + 1)
                for t in range(TC):
                    xt = x_sb[:, i * TC + t, :]
                    last = nc.vector.tensor_scalar(xt, xt, mv0[:, t, 0:1], 0.0, ALU.subtract, ALU.max)
                last.then_inc(relu0_ok, 1)

            def h_1(i, src):
                dve.wait_ge(rstd0_ok, i + 1)
                for t in range(TC):
                    k = i * TC + t
                    last = nc.vector.scalar_tensor_tensor(out=nres[:, k, :], in0=tiles(src)[:, t, :],
                                                          scalar=rstd0[:, k:k + 1], in1=b_bc[:, 0, :],
                                                          op0=ALU.mult, op1=ALU.add)
                last.then_inc(h1_ok, 1)

            def read_spare(use):
                kind, i, j, n, engine = USES[use]
                if engine != "dve":
                    return
                dve.wait_ge(spare_filled, use + 1)
                src = bank[NA + use % SPARE]
                if kind == "h1":
                    h_1(i, src[:, :])
                    dve.wait_ge(h1_ok, i + 1)
                    nc.vector.memset(tick[:, :], 0.0).then_inc(read_by["dve"], 1)
                else:
                    nc.vector.tensor_scalar(adj8[:, i, j * P:(j + n) * P], src[:, 0:n * P], 0.0, 0.0, ALU.add, ALU.add,
                                            accum_out=rs_part[:, i, 2 + j // TC:3 + j // TC],
                                            saturate=False).then_inc(read_by["dve"], 1)

            def low_1(k):
                dve.wait_ge(hi1_ok, k + 1)
                nc.vector.scalar_tensor_tensor(out=hs_a[:, k, 1, :], in0=nres[:, k, :], scalar=dinv_in[:, k:k + 1],
                                               in1=hs_a[:, k, 0, :], op0=ALU.mult, op1=ALU.subtract,
                                               accum_out=evidence[:, EV_LO + k:EV_LO + k + 1]).then_inc(lo1_ok, 1)

            dve.wait_ge(ident_ok, 1)
            nc.vector.tensor_copy(ident8[:, :], ident[:, :], saturate=False).then_inc(const_ok, 1)
            dve.wait_ge(parts_zero, 1)
            for k in range(T):
                if k == T - 5:
                    dve.wait_ge(read_by["act"], reads("act", USES_OF[k][0] - 1))
                uses, units = USES_OF[k], UPPER_OF[k]
                half = (len(uses) + 1) // 2
                check(units[0])
                if k == 0:
                    norm_x(0)
                for use in uses[:half]:
                    read_spare(use)
                if k >= SCALED:
                    low_1(k - SCALED)
                for u in units[1:]:
                    check(u)
                for use in uses[half:]:
                    read_spare(use)
                if k == 0:
                    norm_x(1)
                    dve.wait_ge(first_in, 32)
                    read_spare(1)
                if k % TC == TC - 1 and k // TC + 2 < NC:
                    norm_x(k // TC + 2)
            for k in range(T - SCALED, T):
                low_1(k)
            dve.wait_ge(dout_ok, 1)
            dve.wait_ge(params_in, 16 * (4 * LAYERS - 2))

            def residual(q):
                l, bk, t0, nt = ITEMS[q]
                dve.wait_ge(back_ps, q + 1)
                if 2 <= q < LAST:
                    dve.wait_ge(n_ok, q - 1)
                y = tiles(yb[:, q % 2, :])
                for t in range(nt):
                    k = t0 + t
                    last = nc.vector.scalar_tensor_tensor(out=y[:, t, :], in0=tiles(bank[bk][:, :])[:, t, :],
                                                          scalar=dinv_out[:, k:k + 1], in1=nres[:, k, :],
                                                          op0=ALU.mult, op1=ALU.add)
                last.then_inc(y_ok, 1)
                dve.wait_ge(y_ok, q + 1)
                for t in range(nt):
                    last = nc.vector.bn_stats(st[:, t, :], y[:, t, :])
                last.then_inc(stat_ok, 1)
                dve.wait_ge(stat_ok, q + 1)
                if q >= 2:
                    dve.wait_ge(rstd_ok, q - 1)
                for t in range(nt):
                    last = nc.vector.bn_aggr(mv[:, q % 2, t, :], st[:, t, :])
                last.then_inc(mv_ok, 1)
                if q < LAST:
                    dve.wait_ge(mv_ok, q + 1)
                    nc.vector.tensor_scalar(nmean[:, q % 2, :], mv[:, q % 2, :, 0], -1.0, None,
                                            ALU.mult).then_inc(nmean_ok, 1)

            def gain(q):
                l, _, _, nt = ITEMS[q]
                y = tiles(yb[:, q % 2, :])[:, 0:nt, :]
                dve.wait_ge(z_ok, q + 1)
                nc.vector.tensor_tensor(y, y, g_bc[:, l:l + 1, :].to_broadcast([P, nt, E]), ALU.mult).then_inc(zg_ok, 1)

            def result(q):
                _, _, t0, nt = ITEMS[q]
                y = tiles(yb[:, q % 2, :])
                dve.wait_ge(rstd_ok, q + 1)
                for t in range(nt):
                    last = nc.vector.tensor_scalar(y[:, t, :], y[:, t, :], mv[:, q % 2, t, 0:1],
                                                   rstd[:, q % 2, t:t + 1], ALU.subtract, ALU.mult)
                last.then_inc(z_ok, 1)
                gain(q)
                dve.wait_ge(zg_ok, q + 1)
                dve.wait_ge(xb_ok, 1)
                nc.vector.tensor_tensor(nres[:, t0:t0 + nt, :], y[:, 0:nt, :], xb[:, t0:t0 + nt, :],
                                        ALU.add).then_inc(n_ok, 1)

            def bias(q):
                l, bk, _, nt = ITEMS[q]
                dve.wait_ge(h_ps, q + 1)
                if q:
                    dve.wait_ge(lo_ok, q)
                nc.vector.tensor_tensor(tiles(hb[:, 0, :]), tiles(bank[bk][:, :]),
                                        b_bc[:, l + 1:l + 2, :].to_broadcast([P, nt, E]), ALU.add).then_inc(h_ok, 1)

            def low(q):
                l, _, t0, nt = ITEMS[q]
                hs = hs_of[l + 1]
                dve.wait_ge(h_ok, q + 1)
                dve.wait_ge(hi_ok, q + 1)
                for t in range(nt):
                    k = t0 + t
                    ev = EV_LO + (l + 1) * T + k
                    last = nc.vector.scalar_tensor_tensor(out=hs[:, k, 1, :], in0=tiles(hb[:, 0, :])[:, t, :],
                                                          scalar=dinv_in[:, k:k + 1], in1=hs[:, k, 0, :],
                                                          op0=ALU.mult, op1=ALU.subtract,
                                                          accum_out=evidence[:, ev:ev + 1])
                last.then_inc(lo_ok, 1)

            def sum_up():
                dve.wait_ge(verified, len(LOWER))
                dve.wait_ge(lo_ok, LAST)
                dve.wait_ge(diag_ok, NC)
                nc.vector.tensor_scalar(evidence[:, EV_LO:EV_END], evidence[:, EV_LO:EV_END], 0.0, None,
                                        ALU.mult).then_inc(ev_step, 1)
                dve.wait_ge(ev_step, 1)
                nc.vector.tensor_reduce(ev_sum[:, :], evidence[:, :], AX.X, ALU.add).then_inc(ev_step, 1)

            def verdict():
                dve.wait_ge(ev_ps, 1)
                nc.vector.tensor_scalar(clean[:, :], bank[0][0:1, 0:1], 0.0, None, ALU.is_equal).then_inc(clean_ok, 1)

            for step, i in VECTOR_STEPS:
                if step == "residual":
                    residual(i)
                elif step == "gain":
                    gain(i)
                elif step == "bias":
                    bias(i)
                elif step == "low":
                    low(i)
                elif step == "result":
                    result(i)
                elif step == "verify":
                    verify(i)
                elif step == "verify_diagonal":
                    verify_diagonal(i)
                elif step == "sum_up":
                    sum_up()
                elif step == "verdict":
                    verdict()
            with unless_clean(dve):
                dve.wait_ge(out_done, 16 * (len(ITEMS) - LAST))
                general_vector(nc, dve, m)

        @block.tensor
        def _(pe):
            def fill_spare(use):
                kind, i, j, n, _ = USES[use]
                if use >= SPARE:
                    engine = USES[use - SPARE][-1]
                    pe.wait_ge(read_by[engine], reads(engine, use - SPARE))
                dst = bank[NA + use % SPARE]
                if kind == "xT":
                    pe.wait_ge(relu0_ok, i + 1)
                    for t in range(TC):
                        last = nc.tensor.transpose(dst[:, t * P:(t + 1) * P], x_sb[:, i * TC + t, :], ident[:, :])
                elif kind == "h1":
                    xT_use = USES.index(("xT", i, 0, TC, "act"))
                    pe.wait_ge(read_by["act"], reads("act", xT_use))
                    for t in range(TC):
                        last = nc.tensor.matmul(dst[:, t * E:(t + 1) * E], xT[:, i % 2, t * P:(t + 1) * P],
                                                w_sb[:, 0, :], start=True, stop=True)
                else:
                    pe.wait_ge(converted, UPPER_OF[j + n - 1][-1] + 1)
                    for t in range(n):
                        last = nc.tensor.matmul(dst[:, t * P:(t + 1) * P], adj8[:, j + t, i * P:(i + 1) * P],
                                                ident8[:, :], start=True, stop=True)
                last.then_inc(spare_filled, 1)

            def product(q, k, part):
                l, bk, t0, nt = ITEMS[q]
                last = nc.tensor.matmul(bank[bk][:, 0:nt * P], hs_of[l][:, k, part, :],
                                        adj8[:, k, t0 * P:(t0 + nt) * P],
                                        start=(k == 0 and part == 0), stop=(k == T - 1 and part == 1))
                if k == T - 1 and part == 1:
                    last.then_inc(acc_done, 1)

            def accumulate(qs, k):
                for part in range(2):
                    for q in qs:
                        product(q, k, part)

            def diagonal(d):
                if d == 0:
                    pe.wait_ge(lo_ok, NC)
                if d >= 2:
                    pe.wait_ge(diag_ok, d - 1)
                for t in range(TC):
                    k = d * TC + t
                    last = nc.tensor.matmul(bank[NC - 2 + d % 2][:, t * P:(t + 1) * P], adj8[:, k, k * P:(k + 1) * P],
                                            ident8[:, :], start=True, stop=True)
                last.then_inc(diag_ps, 1)

            def back(q):
                _, bk, _, nt = ITEMS[q]
                pe.wait_ge(relu_ok, q + 1)
                for t in range(nt):
                    last = nc.tensor.transpose(bank[bk][:, t * P:(t + 1) * P], reluT[:, q % 2, t * P:(t + 1) * P],
                                               ident[:, :])
                last.then_inc(back_ps, 1)

            def transpose_n(q):
                _, bk, t0, nt = ITEMS[q]
                pe.wait_ge(n_ok, q + 1)
                for t in range(nt):
                    last = nc.tensor.transpose(bank[bk][:, t * P:(t + 1) * P], nres[:, t0 + t, :], ident[:, :])
                last.then_inc(nT_ps, 1)

            def project(q):
                l, bk, _, nt = ITEMS[q]
                pe.wait_ge(nT_ok, q + 1)
                for t in range(nt):
                    last = nc.tensor.matmul(bank[bk][:, t * E:(t + 1) * E], nT[:, 0, t * P:(t + 1) * P],
                                            w_sb[:, l + 1, :], start=True, stop=True)
                last.then_inc(h_ps, 1)

            pe.wait_ge(ident_ok, 1)
            fill_spare(0)
            pe.wait_ge(first_in, 32)
            fill_spare(1)
            pe.wait_ge(const_ok, 1)
            for k in range(T + BEHIND):
                uses = USES_OF[k] if k < T else []
                at_once = AT_ONCE if k >= BEHIND else len(uses)
                for use in uses[:at_once]:
                    fill_spare(use)
                uses = uses[at_once:]
                if k < BEHIND:
                    continue
                pe.wait_ge(lo1_ok, k - BEHIND + 1)
                turns = [(n + 1) * 2 * NA // (len(uses) + 1) for n in range(len(uses))]
                n_mm = 0
                for part in range(2):
                    for q in range(NA):
                        for use, turn in zip(uses, turns):
                            if turn == n_mm:
                                fill_spare(use)
                        product(q, k - BEHIND, part)
                        n_mm += 1

            g = 0

            def products(qs, k):
                nonlocal g
                accumulate(qs, k)
                for _ in qs:
                    g += 1
                    for step, i in TENSOR_DUE.get(g, ()):
                        if step == "back":
                            back(i)
                        elif step == "transpose_n":
                            transpose_n(i)
                        elif step == "project":
                            project(i)
                        elif step == "diagonal":
                            diagonal(i)

            for q in range(NA, NC):
                if q == NA:
                    pe.wait_ge(params_in, 16 * (4 * LAYERS - 2))
                    for engine in ("act", "dve"):
                        pe.wait_ge(read_by[engine], reads(engine, len(USES)))
                for k in range(T):
                    products([q], k)
            for e in range(NC):
                pe.wait_ge(lo_ok, e + 1)
                for k in range(e * TC, (e + 1) * TC):
                    if e:
                        products(list(range(NC, NC + min(e, WIDE))), k)
                if e < WIDE:
                    for k in range((e + 1) * TC):
                        products([NC + e], k)
            for q in range(NC + WIDE, LAST):
                if ITEMS[q][1] == NC - 2:
                    pe.wait_ge(diag_ok, NC)
                for k in range(T):
                    products([q], k)
            for k in range(T):
                if k % TC == 0:
                    pe.wait_ge(lo_ok, NC + k // TC + 1)
                products([LAST, LAST + 1], k)
            for q in range(LAST + 2, len(ITEMS)):
                if q == len(ITEMS) - 1:
                    pe.wait_ge(y_ok, q - 2)
                for k in range(T):
                    products([q], k)
            assert g > max(TENSOR_DUE), "every step was due within the stream"
            back(len(ITEMS) - 1)
            pe.wait_ge(ev_step, 2)
            nc.tensor.matmul(bank[0][0:1, 0:1], ev_sum[:, :], ones[:, :], start=True, stop=True).then_inc(ev_ps, 1)
            with unless_clean(pe):
                general_tensor(nc, pe, m)


_PARAMS = ["W", "b", "g", "be"]


def kernel(**inputs):
    import numpy as _np
    import concourse.bacc as _bacc
    from concourse import mybir as _mybir
    from concourse.bass_utils import run_bass_kernel_spmd as _run

    nc = _bacc.Bacc("TRN2", target_bir_lowering=False, num_devices=1)
    arrays, aps = {}, {}
    for name in ["x", "adj"] + [f"L0_gnn_{p}{l + 1}" for p in _PARAMS for l in range(LAYERS)]:
        a = _np.ascontiguousarray(inputs[name])
        arrays[f"in_{name}"] = a
        aps[name] = nc.dram_tensor(f"in_{name}", a.shape, _mybir.dt.from_np(a.dtype), kind="ExternalInput").ap()
    out = nc.dram_tensor("out_0", (N, E), _mybir.dt.float32, kind="ExternalOutput").ap()
    w, b, g, be = ([aps[f"L0_gnn_{p}{l + 1}"] for l in range(LAYERS)] for p in _PARAMS)
    build(nc, aps["x"], aps["adj"], w, b, g, be, out)
    r = _run(nc, [arrays], core_ids=[0])
    return r.results[0]["out_0"]
```
